# Optimizing a Trainium2 kernel written in Bass

```python
import numpy as np
import jax
import jax.numpy as jnp

def _softmax(x, axis=-1):
    return jax.nn.softmax(x, axis=axis)

def _gelu(x):
    return jax.nn.gelu(x, approximate=True)

def _silu(x):
    return jax.nn.silu(x)

def _sigmoid(x):
    return jax.nn.sigmoid(x)

def _layernorm(x, axis=-1, eps=1e-05):
    m = jnp.mean(x, axis=axis, keepdims=True)
    v = jnp.var(x, axis=axis, keepdims=True)
    return (x - m) / jnp.sqrt(v + eps)

def _scatter_add(tgt, idx, src, axis=0):
    return tgt.at[idx].add(src)

def _segment_sum(src, seg, n):
    return jax.ops.segment_sum(src, seg, n)
kernel_name = 'mk_adj_preln_d1_adj_r2_0e4020'

def setup_inputs(seed: int=0):
    np.random.seed(seed)
    _w = jnp.asarray

    def _rec_inputs():
        import jax
        import jax.numpy as jnp
        _gk = jax.random.key(seed)
        x = -0.000929 + 1 * jax.random.normal(jax.random.fold_in(_gk, 1), (8192, 128), jnp.float32)
        _a = jax.random.bernoulli(jax.random.fold_in(_gk, 2), 0.000976562, (8192, 8192))
        _a = jnp.logical_or(_a, jnp.swapaxes(_a, -1, -2))
        _a = jnp.logical_or(_a, jnp.eye(8192, dtype=bool))
        _af = _a.astype(jnp.float32)
        adj = _af
        return (x, adj)
    x, adj = _rec_inputs()

    def _L0_gnn_setup():
        import jax, jax.numpy as jnp
        import numpy as np
        ALPHA = 0.2
        NEG_INF = -9000000000000000.0
        LN_EPS = 1e-05
        N = 2048
        IN_F = 128
        OUT_F = 128
        HEADS = 4
        HEAD_DIM = OUT_F // HEADS
        EDGE_PROB = 0.02
        key = jax.random.key(seed)
        kx, ka, kw, kav = jax.random.split(key, 4)
        x = jax.random.normal(kx, (N, IN_F), dtype=jnp.float32)
        adj = jax.random.bernoulli(ka, EDGE_PROB, (N, N)).astype(jnp.float32)
        adj = jnp.maximum(adj, jnp.eye(N, dtype=jnp.float32))

        def xavier(k, shape, gain=1.414):
            fan_in, fan_out = (shape[0], shape[1])
            bound = gain * np.sqrt(6.0 / (fan_in + fan_out))
            return jax.random.uniform(k, shape, jnp.float32, -bound, bound)
        W = xavier(kw, (IN_F, OUT_F))
        a = xavier(kav, (2 * HEAD_DIM, 1))
        gamma = jnp.ones((OUT_F,), dtype=jnp.float32)
        beta = jnp.zeros((OUT_F,), dtype=jnp.float32)
        return {'x': x, 'adj': adj, 'W': W, 'a': a, 'gamma': gamma, 'beta': beta}
    _L0_gnn_all = _L0_gnn_setup()
    _L0_gnn_in = {k: v for k, v in _L0_gnn_all.items() if k in ('W', 'a', 'gamma', 'beta')}
    del _L0_gnn_all
    return {'x': x, 'adj': adj, 'L0_gnn_W': _L0_gnn_in['W'], 'L0_gnn_a': _L0_gnn_in['a'], 'L0_gnn_gamma': _L0_gnn_in['gamma'], 'L0_gnn_beta': _L0_gnn_in['beta']}

def reference(x, adj, L0_gnn_W, L0_gnn_a, L0_gnn_gamma, L0_gnn_beta):
    import jax
    import jax.numpy as jnp

    def _L0_gnn_ref(x, adj, W, a, gamma, beta):
        import jax, jax.numpy as jnp
        import numpy as np
        ALPHA = 0.2
        NEG_INF = -9000000000000000.0
        LN_EPS = 1e-05
        N = 2048
        IN_F = 128
        OUT_F = 128
        HEADS = 4
        HEAD_DIM = OUT_F // HEADS
        EDGE_PROB = 0.02
        n = x.shape[0]
        head_dim = a.shape[0] // 2
        heads = W.shape[1] // head_dim
        h = (x @ W).reshape(n, heads, head_dim)
        src = jnp.einsum('nhd,d->nh', h, a[:head_dim, 0])
        dst = jnp.einsum('nhd,d->nh', h, a[head_dim:, 0])
        e = src[:, :, None] + dst.T[None, :, :]
        e = jnp.where(e > 0, e, ALPHA * e)
        mask = adj[:, None, :] > 0
        e = jnp.where(mask, e, NEG_INF)
        attn = jax.nn.softmax(e, axis=-1)
        out = jnp.einsum('nhm,mhd->nhd', attn, h)
        out = out.reshape(n, heads * head_dim)
        mu = jnp.mean(out, axis=-1, keepdims=True)
        var = jnp.var(out, axis=-1, keepdims=True)
        out = (out - mu) / jnp.sqrt(var + LN_EPS) * gamma + beta
        return out
    h = jnp.maximum(_layernorm(x, axis=-1), 0.0)
    x = x + _L0_gnn_ref(h, adj, L0_gnn_W, L0_gnn_a, L0_gnn_gamma, L0_gnn_beta)
    return x

_drawn_inputs = setup_inputs


def setup_inputs(seed=0):
    import zlib

    import numpy as np

    out = dict(_drawn_inputs(seed))
    spreads = {'L0_gnn_gamma': (1.0, 0.2), 'L0_gnn_beta': (0.0, 0.1)}
    factors = {}
    for name, (base, spread) in spreads.items():
        noise = np.random.default_rng([zlib.crc32(name.encode()), seed]).standard_normal(out[name].shape)
        drawn = base * np.exp(spread * noise) if base else spread * noise
        out[name] = jnp.asarray(drawn.astype(out[name].dtype))
    for name, factor in factors.items():
        out[name] = (out[name] * factor).astype(out[name].dtype)
    return out
```

```python
import math

import concourse.bass as bass
from concourse import mybir
from contextlib import ExitStack

RMAX = bass.bass_isa.ReduceOp.max


def bass_gat_preln_kernel(nc, x, adj, W, a, gamma, beta, out):
    fp32 = mybir.dt.float32
    bf16 = mybir.dt.bfloat16
    fp16 = mybir.dt.float16
    ALU = mybir.AluOpType
    ACT = mybir.ActivationFunctionType
    AX = mybir.AxisListType

    P = 128
    N, F = x.shape
    HD = a.shape[0] // 2
    H = W.shape[1] // HD
    HA = HD + 1
    NT = N // P
    EPS = 1e-5
    SLOPE = 0.2

    PG = 8
    PSTEPS = NT // PG

    IB = 4
    BI = IB * P
    BLOCKS = N // BI
    CJ = 2
    LJ = 4
    NBUF = 4
    CPL = LJ // CJ
    BODY = NBUF * CPL
    CHUNKS = NT // CJ
    BODIES = CHUNKS // BODY
    WC = 4 * HA
    SCALE = 10 * math.log(2.0)
    LO = 2048.0
    ZH = H - 1

    ctx = ExitStack()
    with ctx:
        def sb(name, shape, dt):
            return ctx.enter_context(nc.sbuf_tensor(name, shape, dt))

        def sem(name):
            return ctx.enter_context(nc.semaphore(name))

        weights = sb("weights", [P, NT, H, WC], fp16)
        adj_in = sb("adj_in", [P, NBUF, IB, LJ * P], fp32)
        maskA = sb("maskA", [P, 2, CJ, BI], fp16)
        maskB = sb("maskB", [P, 2, H, CJ, BI], fp16)
        below = sb("below", [P, 2, ZH, CJ, BI], bf16)
        s_rows = sb("s_rows", [P, 2, H, BI], fp32)
        hbig = sb("hbig", [P, NT * H * HA], fp32)
        haug = hbig[:, :].rearrange("p (t h c) -> p t h c", h=H, c=HA)
        sd = sb("sd", [P, 2 * H, NT], fp32)
        negd = sb("negd", [P, NT, H], fp32)
        coefU = sb("coefU", [P, NT, H], fp32)
        coefV = sb("coefV", [P, NT, H], fp32)
        expU = sb("expU", [P, NT, H], fp32)
        expV = sb("expV", [P, NT, H], fp32)
        ident = sb("ident", [P, P], fp32)
        ident16 = sb("ident16", [P, P], bf16)
        ones = sb("ones", [P, P], fp32)
        zero16 = sb("zero16", [1, 512], fp16)
        gam = sb("gam", [P, F], fp32)
        bet = sb("bet", [P, F], fp32)
        small = sb("small", [P, 64], fp32)
        hsum = sb("hsum", [P, H * HA], fp32)

        zf = below[:, :, :, :, :].bitcast(fp32).rearrange("p a b c d -> p (a b c d)")
        bf = maskB[:, :, :, :, :].bitcast(fp32).rearrange("p a b c d -> p (a b c d)")
        xin = bf[:, 0:2 * PG * F].rearrange("p (s t f) -> p s t f", s=2, f=F)
        hn = bf[:, 2 * PG * F:4 * PG * F].rearrange("p (s t f) -> p s t f", s=2, f=F)
        hnT = zf[:, 0:PG * P].rearrange("p (t n) -> p t n", n=P)
        o = PG * P
        Wsb = zf[:, o:o + F]
        WT = zf[:, o + F:o + 2 * F]
        WA = zf[:, o + 2 * F:o + 2 * F + 2 * H]
        Asd = zf[:, o + 2 * F + 2 * H:o + 2 * F + 4 * H]
        o += 2 * F + 4 * H
        stats = zf[:, o:o + PG * 6].rearrange("p (t c) -> p t c", c=6)
        mv = zf[:, o + PG * 6:o + PG * 10].rearrange("p (s t c) -> p s t c", s=2, c=2)
        o += PG * 10
        rstd = zf[:, o:o + 2 * PG].rearrange("p (s t) -> p s t", s=2)
        nmr = zf[:, o + 2 * PG:o + 4 * PG].rearrange("p (s t) -> p s t", s=2)
        vpe = zf[:, o + 4 * PG:o + 5 * PG]
        gate = sb("gate", [P, 1], fp32)
        epsc = sb("epsc", [P, PG], fp32)[:, :]
        inv_lo = sb("inv_lo", [P, 1], fp32)[:, :]
        expo = small[:, 48:56]
        mone = small[:, 32:48]
        o += 5 * PG
        assert o <= zf.shape[1]
        WG = 4
        WSTEPS = NT // WG
        XN = WG * H * HA
        xw = [bf[:, k * XN:(k + 1) * XN].rearrange("p (t h c) -> p t h c", h=H, c=HA) for k in range(2)]
        srow_st = bf[:, 2 * XN:2 * XN + 2 * P].rearrange("p (k n) -> p k n", n=P)
        o = 2 * XN + 2 * P
        yv = bf[:, o:o + 2 * NT * H].rearrange("p (k h t) -> p k h t", h=H, k=2)
        o += 2 * NT * H
        hpart = bf[:, o:o + H * HA]

        e = 0
        acc_sb = hbig[:, 0:IB * H * WC].rearrange("p (i h c) -> p i h c", h=H, c=WC)
        e += IB * H * WC
        uu = hbig[:, e:e + IB * H * HA].rearrange("p (i h c) -> p i h c", h=H, c=HA)
        e += IB * H * HA
        vv = hbig[:, e:e + IB * H * HA].rearrange("p (i h c) -> p i h c", h=H, c=HA)
        e += IB * H * HA
        feat = hbig[:, e:e + IB * F].rearrange("p (i f) -> p i f", f=F)
        e += IB * F
        tree = hbig[:, e:e + IB * F].rearrange("p (i f) -> p i f", f=F)
        e += IB * F
        x_res = hbig[:, e:e + 2 * IB * F].rearrange("p (s i f) -> p s i f", s=2, f=F)
        e += 2 * IB * F
        yout = hbig[:, e:e + IB * F].rearrange("p (i f) -> p i f", f=F)
        e += IB * F
        sq = hbig[:, e:e + IB * F].rearrange("p (i f) -> p i f", f=F)
        e += IB * F
        lnst = hbig[:, e:e + 8 * IB].rearrange("p (k i) -> p k i", i=IB)
        e += 8 * IB
        e0 = hbig[:, e:e + IB * H].rearrange("p (i h) -> p i h", h=H)
        e += IB * H
        assert e <= NT * H * HA

        bank = [ctx.enter_context(nc.psum_tensor(f"bank{i}", [P, 512], fp32)) for i in range(8)]
        ptr = [bank[0], bank[1]]
        ph = [bank[2], bank[3]]
        psd = bank[4]
        pmisc = bank[5]
        accA = [bank[i][:, 0:3 * WC].rearrange("p (h c) -> p h c", c=WC) for i in range(IB)]
        accB = [bank[4 + i][:, 0:2 * WC].rearrange("p (i c) -> p i c", c=WC) for i in range(IB // 2)]
        turned = [bank[6 + s][:, :].bitcast(bf16).rearrange("p (u i) -> p u i", i=BI) for s in range(2)]

        def acc(it, h):
            return accA[it][:, h, :] if h < 3 else accB[it // 2][:, it % 2, :]

        s_dram = nc.dram_tensor("s_scratch", [H, N], fp32, kind="Internal").ap()

        consts_loaded = sem("consts_loaded")
        a_loaded = sem("a_loaded")
        consts_made = sem("consts_made")
        asd_clear = sem("asd_clear")
        wt_turned = sem("wt_turned")
        wt_copied = sem("wt_copied")
        wa_made = sem("wa_made")
        wa_copied = sem("wa_copied")
        x_loaded = [sem(f"x_loaded{i}") for i in range(2)]
        stats_made = sem("stats_made")
        moments_made = sem("moments_made")
        norm_made = sem("norm_made")
        hn_made = sem("hn_made")
        hn_turned = sem("hn_turned")
        hnT_copied = sem("hnT_copied")
        h_made = sem("h_made")
        h_copied = sem("h_copied")
        s_turned = sem("s_turned")
        s_copied = sem("s_copied")
        s_stored = sem("s_stored")
        col_max = sem("col_max")
        all_max = sem("all_max")
        bias_made = sem("bias_made")
        exps_made = sem("exps_made")
        expU_negated = sem("expU_negated")
        y_made = sem("y_made")
        coefs_made = sem("coefs_made")
        scaled = sem("scaled")
        hi_made = sem("hi_made")
        rest_made = sem("rest_made")
        lo_made = sem("lo_made")
        hsum_part = sem("hsum_part")
        hsum_made = sem("hsum_made")
        hsum_copied = sem("hsum_copied")
        adj_loaded = [sem(f"adj_loaded{i}") for i in range(NBUF)]
        rows_loaded = [sem(f"rows_loaded{i}") for i in range(2)]
        tile_turned = sem("tile_turned")
        maskA_made = sem("maskA_made")
        below_made = sem("below_made")
        masks_made = sem("masks_made")
        masks_used = sem("masks_used")
        acc_copied = sem("acc_copied")
        acc_read = sem("acc_read")
        pool_step = sem("pool_step")
        y_stored = sem("y_stored")

        block = ctx.enter_context(nc.Block())

        @block.sync
        def _(sp):
            sp.dma_start(Wsb, W).then_inc(consts_loaded, 16)
            sp.dma_start(gam[:, :], gamma.partition_broadcast(P)).then_inc(consts_loaded, 16)
            sp.dma_start(bet[:, :], beta.partition_broadcast(P)).then_inc(consts_loaded, 16)
            x_v = x.rearrange("(t p) f -> p t f", p=P)
            with sp.Fori(0, PSTEPS // 2) as n:
                for s in range(2):
                    sp.wait_ge(hn_made, n * 2 + (s + 1))
                    sp.dma_start(xin[:, s], x_v[:, bass.ds(n * (2 * PG) + s * PG, PG), :]).then_inc(x_loaded[s], 16)
            sp.wait_ge(s_copied, 1)
            sp.dma_start(s_dram.rearrange("(k h) (t p) -> (h t) k p", p=P, k=2), srow_st).then_inc(s_stored, 16)
            sp.wait_ge(s_stored, 16)
            adj_v = adj.rearrange("(b i p) j -> b p i j", i=IB, p=P)
            xr_v = x.rearrange("(b i p) f -> b p i f", i=IB, p=P)

            def block_loads(b, half):
                sp.wait_ge(acc_read, b + 1)
                sp.dma_start(s_rows[:, half], s_dram[:, bass.ds(b * BI, BI)].partition_broadcast(P)).then_inc(rows_loaded[half], 16)
                sp.dma_start(x_res[:, half], xr_v[b]).then_inc(rows_loaded[half], 16)
                with sp.Fori(0, BODIES) as q:
                    for k in range(NBUF):
                        sp.wait_ge(tile_turned, (b * BODIES + q) * BODY + (k + 1) * CPL)
                        sp.dma_start(adj_in[:, k], adj_v[b][:, :, bass.ds(q * (NBUF * LJ * P) + k * LJ * P, LJ * P)]).then_inc(adj_loaded[k], 16)

            sp.wait_ge(hsum_copied, 1)
            with sp.Fori(0, BLOCKS // 2) as bp:
                for half in range(2):
                    block_loads(bp * 2 + half, half)

        @block.gpsimd
        def _(pool):
            def chain():
                count = [0]

                def step(ins):
                    count[0] += 1
                    ins.then_inc(pool_step, 1)
                    pool.wait_ge(pool_step, count[0])
                return step

            pool.sem_inc(norm_made, 1)
            nc.gpsimd.memset(Asd, 0.0).then_inc(asd_clear, 1)
            nc.gpsimd.memset(ones[:, :], 1.0)
            nc.gpsimd.memset(zero16[:, :], 0.0)
            nc.gpsimd.memset(expo, -0.5)
            nc.gpsimd.memset(mone, -1.0)
            nc.gpsimd.memset(epsc, EPS)
            nc.gpsimd.memset(inv_lo, 1.0 / LO)
            nc.gpsimd.memset(haug[:, :, :, HD:HA], 1.0)
            nc.gpsimd.memset(ident[:, :], 0.0).then_inc(pool_step, 1)
            pool.wait_ge(pool_step, 1)
            nc.gpsimd.affine_select(out=ident[:, :], in_=ident[:, :], compare_op=ALU.not_equal, fill=1.0,
                                    base=0, pattern=[[-1, P]], channel_multiplier=1).then_inc(pool_step, 1)
            pool.wait_ge(pool_step, 2)
            pool.sem_clear(pool_step)
            nc.gpsimd.tensor_copy(ident16[:, :], ident[:, :]).then_inc(consts_made, 1)
            pool.wait_ge(asd_clear, 1)
            a_v = a.rearrange("(k d) o -> k d o", k=2)
            for h in range(H):
                for k in range(2):
                    pool.dma_start(Asd[h * HD:(h + 1) * HD, k * H + h:k * H + h + 1], a_v[k]).then_inc(a_loaded, 16)
            with pool.Fori(0, PSTEPS // 2) as n:
                for s in range(2):
                    st = n * 2 + s
                    pool.wait_ge(moments_made, st + 1)
                    pool.wait_ge(hn_made, st + 1)
                    step = chain()
                    step(nc.gpsimd.tensor_tensor(vpe, mv[:, s, :, 1], epsc, ALU.add))
                    step(nc.gpsimd.tensor_tensor(rstd[:, s], vpe, expo, ALU.pow))
                    step(nc.gpsimd.tensor_tensor(nmr[:, s], mv[:, s, :, 0], rstd[:, s], ALU.mult))
                    pool.sem_clear(pool_step)
                    nc.gpsimd.tensor_scalar(nmr[:, s], nmr[:, s], -1.0, None, ALU.mult).then_inc(norm_made, 1)
            pool.wait_ge(col_max, 3)
            nc.gpsimd.partition_all_reduce(small[:, 16:16 + 2 * H + 1], small[:, 0:2 * H + 1], P, RMAX).then_inc(all_max, 1)

            pool.wait_ge(hsum_copied, 1)
            pool.wait_ge(coefs_made, 1)
            pool.wait_ge(consts_loaded, 48)
            pool.sem_inc(acc_read, 2)
            out_v = out.rearrange("(b i p) f -> b p i f", i=IB, p=P)
            hs_b = hsum[:, :].rearrange("p (h c) -> p h c", c=HA).unsqueeze(1).broadcast_to([P, IB, H, HA])

            def over(ap, n):
                return ap.unsqueeze(len(ap.shape)).broadcast_to(list(ap.shape) + [n])

            def tree_sum(src, dst, step):
                w = F // 2
                step(nc.gpsimd.tensor_tensor(tree[:, :, 0:w], src[:, :, 0:w], src[:, :, w:F], ALU.add))
                while w > 2:
                    w //= 2
                    step(nc.gpsimd.tensor_tensor(tree[:, :, 0:w], tree[:, :, 0:w], tree[:, :, w:2 * w], ALU.add))
                step(nc.gpsimd.tensor_tensor(dst, tree[:, :, 0], tree[:, :, 1], ALU.add))

            with pool.Fori(0, BLOCKS // 2) as bp:
                for half in range(2):
                    b = bp * 2 + half
                    pool.wait_ge(acc_copied, b * 2 + 4)
                    pool.wait_ge(rows_loaded[half], bp * 32 + 32)
                    cu = over(coefU[:, bass.ds(b * IB, IB), :], HA)
                    cv = over(coefV[:, bass.ds(b * IB, IB), :], HA)

                    def part(k):
                        return acc_sb[:, :, :, k * HA:(k + 1) * HA]

                    step = chain()
                    nc.gpsimd.tensor_tensor(uu, part(1), inv_lo.unsqueeze(2).unsqueeze(3).broadcast_to([P, IB, H, HA]), ALU.mult)
                    step(nc.gpsimd.tensor_scalar(vv, part(3), 1.0 / LO, None, ALU.mult))
                    nc.gpsimd.tensor_tensor(uu, uu, part(0), ALU.add)
                    step(nc.gpsimd.tensor_tensor(vv, vv, part(2), ALU.add))
                    nc.gpsimd.tensor_tensor(uu, uu, cu, ALU.mult)
                    step(nc.gpsimd.tensor_tensor(vv, vv, cv, ALU.mult))
                    step(nc.gpsimd.tensor_tensor(uu, uu, vv, ALU.add))
                    step(nc.gpsimd.tensor_scalar(e0, uu[:, :, :, HD], 0.0, None, ALU.is_equal))
                    step(nc.gpsimd.tensor_tensor(vv, hs_b, over(e0, HA), ALU.mult))
                    step(nc.gpsimd.tensor_tensor(uu, uu, vv, ALU.add))
                    step(nc.gpsimd.tensor_tensor(e0, uu[:, :, :, HD], mone.rearrange("p (i h) -> p i h", h=H), ALU.pow))
                    step(nc.gpsimd.tensor_tensor(feat.rearrange("p i (h c) -> p i h c", c=HD), uu[:, :, :, 0:HD],
                                                 over(e0, HD), ALU.mult))
                    tree_sum(feat, lnst[:, 0], step)
                    step(nc.gpsimd.tensor_scalar(lnst[:, 1], lnst[:, 0], 1.0 / F, None, ALU.mult))
                    step(nc.gpsimd.tensor_tensor(feat, feat, over(lnst[:, 1], F), ALU.subtract))
                    step(nc.gpsimd.tensor_tensor(sq, feat, feat, ALU.mult))
                    tree_sum(sq, lnst[:, 2], step)
                    step(nc.gpsimd.tensor_scalar(lnst[:, 3], lnst[:, 2], 1.0 / F, EPS, ALU.mult, ALU.add))
                    step(nc.gpsimd.tensor_tensor(lnst[:, 4], lnst[:, 3], expo[:, 0:IB], ALU.pow))
                    step(nc.gpsimd.tensor_tensor(feat, feat, over(lnst[:, 4], F), ALU.mult))
                    step(nc.gpsimd.tensor_tensor(feat, feat, gam[:, :].unsqueeze(1).broadcast_to([P, IB, F]), ALU.mult))
                    step(nc.gpsimd.tensor_tensor(feat, feat, bet[:, :].unsqueeze(1).broadcast_to([P, IB, F]), ALU.add))
                    pool.sem_clear(pool_step)
                    nc.gpsimd.tensor_tensor(yout, feat, x_res[:, half], ALU.add).then_inc(acc_read, 1)
                    pool.wait_ge(acc_read, b + 3)
                    pool.dma_start(out_v[b], yout).then_inc(y_stored, 16)
                    pool.wait_ge(y_stored, b * 16 + 16)

        @block.vector
        def _(dve):
            dve.sem_inc(lo_made, 2)
            dve.sem_inc(masks_made, 2)
            dve.sem_inc(maskA_made, 1)

            dve.wait_ge(wt_turned, 1)
            nc.vector.tensor_copy(WT, pmisc[:, 0:F]).then_inc(wt_copied, 1)
            dve.wait_ge(wa_made, 1)
            nc.vector.tensor_copy(WA, pmisc[:, F:F + 2 * H]).then_inc(wa_copied, 1)

            def layer_stats(st, s, loads):
                dve.wait_ge(x_loaded[s], loads)
                dve.wait_ge(moments_made, st)
                for t in range(PG):
                    last = nc.vector.bn_stats(stats[:, t], xin[:, s, t])
                last.then_inc(stats_made, 1)
                dve.wait_ge(stats_made, st + 1)
                if isinstance(st, int) and st == 0:
                    pass
                else:
                    dve.wait_ge(norm_made, st)
                nc.vector.memset(gate[:, :], 0.0)
                for t in range(PG):
                    last = nc.vector.bn_aggr(mv[:, s, t], stats[:, t])
                last.then_inc(moments_made, 1)

            def copy_turned(st):
                dve.wait_ge(hn_turned, st + 3)
                dve.wait_ge(h_made, st + 1)
                for i in range(2):
                    last = nc.vector.tensor_copy(hnT[:, 4 * i:4 * i + 4], ptr[i][:, :].rearrange("p (t n) -> p t n", n=P))
                last.then_inc(hnT_copied, 1)

            layer_stats(0, 0, 16)
            with dve.Fori(0, PSTEPS // 2 - 1) as n:
                layer_stats(n * 2 + 1, 1, n * 16 + 16)
                copy_turned(n * 2)
                layer_stats(n * 2 + 2, 0, n * 16 + 32)
                copy_turned(n * 2 + 1)
            layer_stats(PSTEPS - 1, 1, 8 * PSTEPS)
            copy_turned(PSTEPS - 2)
            copy_turned(PSTEPS - 1)

            dve.wait_ge(h_copied, PSTEPS + 1)
            nc.vector.tensor_reduce(small[:, 0:H], sd[:, H:2 * H, :], axis=AX.X, op=ALU.max).then_inc(col_max, 1)
            nc.vector.tensor_reduce(small[:, H:2 * H], sd[:, H:2 * H, :], axis=AX.X, op=ALU.min, negate=True).then_inc(col_max, 1)
            nc.vector.tensor_reduce(small[:, 2 * H:2 * H + 1], haug[:, :, :, 0:HD], axis=AX.XYZ, op=ALU.max,
                                    apply_absolute_value=True).then_inc(col_max, 1)
            dve.wait_ge(s_turned, 1)
            nc.vector.tensor_copy(srow_st, pmisc[:, 0:2 * P].rearrange("p (k n) -> p k n", n=P)).then_inc(s_copied, 1)
            nc.vector.tensor_scalar(negd[:, :, :].rearrange("p t h -> p h t"), sd[:, H:2 * H, :], -1.0, None, ALU.mult)
            dve.wait_ge(all_max, 1)
            nc.vector.tensor_scalar(small[:, 56:60], small[:, 16:16 + H], -1.0, SCALE, ALU.mult, ALU.add)
            nc.vector.tensor_scalar(small[:, 60:64], small[:, 16:16 + H], -SLOPE, SCALE, ALU.mult, ALU.add).then_inc(bias_made, 1)
            for h in range(H):
                nc.vector.tensor_scalar(yv[:, 0, h], sd[:, h, :], small[:, 16 + h:17 + h], 0.0, ALU.add, ALU.min)
                last = nc.vector.tensor_scalar(yv[:, 1, h], sd[:, h, :], small[:, 16 + h:17 + h], 0.0, ALU.add, ALU.max)
            last.then_inc(y_made, 1)
            dve.wait_ge(exps_made, 1)
            nc.vector.tensor_scalar(expU[:, :, :], expU[:, :, :], -1.0, None, ALU.mult).then_inc(expU_negated, 1)
            dve.wait_ge(expU_negated, 1)

            with dve.Fori(0, WSTEPS) as g:
                for k, ex in enumerate((expU, expV)):
                    dve.wait_ge(lo_made, g * 2 + (k + 1))
                    nc.vector.tensor_tensor(xw[k], haug[:, bass.ds(g * WG, WG)],
                                            ex[:, bass.ds(g * WG, WG), :].unsqueeze(3).broadcast_to([P, WG, H, HA]),
                                            ALU.mult).then_inc(scaled, 1)
                for k in range(2):
                    dve.wait_ge(hi_made, g * 2 + (k + 1))
                    nc.vector.tensor_tensor(xw[k], xw[k], weights[:, bass.ds(g * WG, WG), :, 2 * k * HA:(2 * k + 1) * HA],
                                            ALU.subtract).then_inc(rest_made, 1)
            nc.vector.tensor_reduce(hpart, hbig[:, :].rearrange("p (t c) -> p c t", t=NT), axis=AX.X, op=ALU.add).then_inc(hsum_part, 1)
            dve.wait_ge(hsum_made, 1)
            nc.vector.tensor_copy(hsum[:, :], pmisc[:, 0:H * HA]).then_inc(hsum_copied, 1)

            dve.wait_ge(lo_made, 2 * WSTEPS + 2)
            dve.wait_ge(coefs_made, 1)
            dve.wait_ge(s_stored, 16)

            def masks(c, slot, half, jt):
                dve.wait_ge(tile_turned, c + (2 * NBUF + 1))
                dve.wait_ge(masks_used, c + 1)
                nc.vector.tensor_scalar(maskA[:, slot], turned[slot], 0.0, 1.0, ALU.is_le, ALU.subtract).then_inc(maskA_made, 1)
                dve.wait_ge(maskA_made, c + 2)
                for u in range(CJ):
                    nc.vector.scalar_tensor_tensor(maskB[:, slot, 0, u], s_rows[:, half, 0], negd[:, bass.ds(jt + u, 1), 0],
                                                   maskA[:, slot, u], ALU.is_lt, ALU.logical_and)
                dve.wait_ge(below_made, c + 1)
                nc.vector.tensor_tensor(maskB[:, slot, H - ZH:H].rearrange("p h u i -> p h (u i)"),
                                        below[:, slot].rearrange("p h u i -> p h (u i)"),
                                        maskA[:, slot].rearrange("p u i -> p (u i)").unsqueeze(1).broadcast_to([P, ZH, CJ * BI]),
                                        ALU.logical_and).then_inc(masks_made, 1)

            def flush(b):
                dve.wait_ge(masks_used, b * CHUNKS + 2)
                dve.wait_ge(acc_read, b + 1)
                nc.vector.tensor_copy(acc_sb[:, 2, 0:3], accA[2])
                nc.vector.tensor_copy(acc_sb[:, 3, 0:3], accA[3])
                nc.vector.tensor_copy(acc_sb[:, 0:2, 3], accB[0]).then_inc(acc_copied, 1)

            with dve.Fori(0, BLOCKS // 2) as bp:
                for half in range(2):
                    b = bp * 2 + half
                    dve.wait_ge(rows_loaded[half], bp * 32 + 32)
                    for k in range(BODY):
                        masks(b * CHUNKS + k, k % 2, half, k * CJ)
                        if k == 0:
                            flush(b)
                    with dve.Fori(1, BODIES) as q:
                        for k in range(BODY):
                            masks((b * BODIES + q) * BODY + k, k % 2, half, q * (BODY * CJ) + k * CJ)
            flush(BLOCKS)

        @block.scalar
        def _(act):
            act.sem_inc(hn_made, 2)
            act.sem_inc(h_copied, 1)

            def normalise(st, s):
                act.wait_ge(norm_made, st + 2)
                act.wait_ge(hn_turned, st + 1)
                for t in range(PG):
                    last = nc.scalar.activation(hn[:, s, t], xin[:, s, t], ACT.Relu,
                                                bias=nmr[:, s, t:t + 1], scale=rstd[:, s, t:t + 1])
                last.then_inc(hn_made, 1)

            def copy_h(st, t0):
                act.wait_ge(h_made, st + 2)
                for i in range(2):
                    nc.scalar.activation(haug[:, bass.ds(t0 + 4 * i, 4), :, 0:HD],
                                         ph[i][:, :].rearrange("p (t h c) -> p t h c", h=H, c=HD), ACT.Copy)
                nc.scalar.activation(sd[:, :, bass.ds(t0, PG)],
                                     psd[:, 0:PG * 2 * H].rearrange("p (t c) -> p c t", c=2 * H), ACT.Copy).then_inc(h_copied, 1)

            act.wait_ge(consts_made, 1)
            normalise(0, 0)
            with act.Fori(0, PSTEPS // 2 - 1) as n:
                normalise(n * 2 + 1, 1)
                copy_h(n * 2, n * (2 * PG))
                normalise(n * 2 + 2, 0)
                copy_h(n * 2 + 1, n * (2 * PG) + PG)
            normalise(PSTEPS - 1, 1)
            copy_h(PSTEPS - 2, NT - 2 * PG)
            copy_h(PSTEPS - 1, NT - PG)

            act.wait_ge(bias_made, 1)
            for h in range(H):
                nc.scalar.activation(expU[:, :, h], sd[:, H + h, :], ACT.Exp, bias=small[:, 56 + h:57 + h])
                last = nc.scalar.activation(expV[:, :, h], sd[:, H + h, :], ACT.Exp, bias=small[:, 60 + h:61 + h], scale=SLOPE)
            last.then_inc(exps_made, 1)
            act.wait_ge(y_made, 1)
            nc.scalar.activation(coefU[:, :, :].rearrange("p t h -> p h t"), yv[:, 0], ACT.Exp, scale=1.0 - SLOPE)
            nc.scalar.activation(coefV[:, :, :].rearrange("p t h -> p h t"), yv[:, 1], ACT.Exp, scale=SLOPE - 1.0).then_inc(coefs_made, 1)
            with act.Fori(0, WSTEPS) as g:
                for k in range(2):
                    act.wait_ge(scaled, g * 2 + (k + 1))
                    nc.scalar.activation(weights[:, bass.ds(g * WG, WG), :, 2 * k * HA:(2 * k + 1) * HA], xw[k],
                                         ACT.Copy).then_inc(hi_made, 1)
                for k in range(2):
                    act.wait_ge(rest_made, g * 2 + (k + 1))
                    nc.scalar.activation(weights[:, bass.ds(g * WG, WG), :, (2 * k + 1) * HA:(2 * k + 2) * HA], xw[k],
                                         ACT.Copy, scale=LO).then_inc(lo_made, 1)

            def compare(c, slot, half, jt):
                act.wait_ge(masks_made, c + 1)
                for u in range(CJ):
                    for z in range(ZH):
                        h = H - ZH + z
                        last = nc.scalar.activation(below[:, slot, z, u], s_rows[:, half, h], ACT.Relu,
                                                    bias=negd[:, bass.ds(jt + u, 1), h], scale=-1.0)
                last.then_inc(below_made, 1)

            def flush(b):
                act.wait_ge(masks_used, b * CHUNKS + 2)
                act.wait_ge(acc_read, b + 1)
                nc.scalar.activation(acc_sb[:, 0, 0:3], accA[0], ACT.Copy)
                nc.scalar.activation(acc_sb[:, 1, 0:3], accA[1], ACT.Copy)
                nc.scalar.activation(acc_sb[:, 2:4, 3], accB[1], ACT.Copy).then_inc(acc_copied, 1)

            act.wait_ge(hsum_copied, 1)
            with act.Fori(0, BLOCKS // 2) as bp:
                for half in range(2):
                    b = bp * 2 + half
                    act.wait_ge(rows_loaded[half], bp * 32 + 32)
                    for k in range(BODY):
                        compare(b * CHUNKS + k, k % 2, half, k * CJ)
                        if k == 1:
                            flush(b)
                    with act.Fori(1, BODIES) as q:
                        for k in range(BODY):
                            compare((b * BODIES + q) * BODY + k, k % 2, half, q * (BODY * CJ) + k * CJ)
            flush(BLOCKS)

        @block.tensor
        def _(pe):
            pe.sem_inc(hn_turned, 2)
            pe.sem_inc(h_made, 1)
            pe.sem_inc(tile_turned, 2 * NBUF)
            pe.wait_ge(consts_made, 1)
            pe.wait_ge(consts_loaded, 48)
            nc.tensor.transpose(pmisc[:, 0:F], Wsb, ident[:, :]).then_inc(wt_turned, 1)
            pe.wait_ge(wt_copied, 1)
            pe.wait_ge(a_loaded, 16 * 2 * H)
            nc.tensor.matmul(pmisc[:, F:F + 2 * H], WT, Asd, start=True, stop=True).then_inc(wa_made, 1)
            pe.wait_ge(wa_copied, 1)

            def turn_rows(st, s):
                pe.wait_ge(hn_made, st + 3)
                pe.wait_ge(hnT_copied, st)
                for t in range(PG):
                    last = nc.tensor.transpose(ptr[t // 4][:, (t % 4) * P:(t % 4 + 1) * P], hn[:, s, t], ident[:, :])
                last.then_inc(hn_turned, 1)

            def project(st):
                pe.wait_ge(hnT_copied, st + 1)
                pe.wait_ge(h_copied, st + 1)
                for t in range(PG):
                    nc.tensor.matmul(ph[t // 4][:, (t % 4) * F:(t % 4 + 1) * F], hnT[:, t], Wsb, start=True, stop=True)
                    last = nc.tensor.matmul(psd[:, t * 2 * H:(t + 1) * 2 * H], hnT[:, t], WA, start=True, stop=True)
                last.then_inc(h_made, 1)

            turn_rows(0, 0)
            with pe.Fori(0, PSTEPS // 2 - 1) as n:
                turn_rows(n * 2 + 1, 1)
                project(n * 2)
                turn_rows(n * 2 + 2, 0)
                project(n * 2 + 1)
            turn_rows(PSTEPS - 1, 1)
            project(PSTEPS - 2)
            project(PSTEPS - 1)
            pe.wait_ge(h_copied, PSTEPS + 1)
            for k in range(2):
                last = nc.tensor.transpose(pmisc[:, k * P:(k + 1) * P], sd[:, 2 * k:2 * k + 2, :].rearrange("p h t -> p (h t)"), ident[:, :])
            last.then_inc(s_turned, 1)
            pe.wait_ge(hsum_part, 1)
            pe.wait_ge(s_copied, 1)
            nc.tensor.matmul(pmisc[:, 0:H * HA], ones[:, :], hpart, start=True, stop=True).then_inc(hsum_made, 1)
            pe.wait_ge(hsum_copied, 1)

            def turn(slot, k, cc):
                a16 = adj_in[:, k].bitcast(bf16)
                for u in range(CJ):
                    for it in range(IB):
                        j0 = 2 * (cc * CJ + u) * P
                        last = nc.tensor.transpose(turned[slot][:, u, it * P:(it + 1) * P],
                                                   a16[:, it, j0 + 1:j0 + 2 * P:2], ident16[:, :])
                last.then_inc(tile_turned, 1)

            def clear():
                for i in range(6):
                    last = nc.tensor.matmul(bank[i][:, :], zero16[0:1, 0:P], zero16[0:1, :], start=True, stop=False,
                                            skip_group_check=True)
                return last

            def products(c, slot, jt):
                pe.wait_ge(masks_made, c + 3)
                for u in range(CJ):
                    w = weights[:, bass.ds(jt + u, 1)].squeeze(1)
                    for it in range(IB):
                        cols = slice(it * P, (it + 1) * P)
                        mA = maskA[:, slot, u, cols]
                        nc.tensor.matmul(accA[it][:, :, 0:2 * HA], mA, w[:, 0:3, 0:2 * HA], start=False, stop=False,
                                         skip_group_check=True)
                        nc.tensor.matmul(accB[it // 2][:, it % 2, 0:2 * HA], mA, w[:, 3, 0:2 * HA], start=False, stop=False,
                                         skip_group_check=True)
                        for h in range(H):
                            last = nc.tensor.matmul(acc(it, h), maskB[:, slot, h, u, cols], w[:, h], start=False, stop=False,
                                                    skip_group_check=True)
                last.then_inc(masks_used, 1)

            def chunk(b, q, k, turn_next=True):
                c = (b * BODIES + q) * BODY + k
                if turn_next:
                    m = (k + 1) % BODY
                    if m % CPL == 0:
                        pe.wait_ge(adj_loaded[m // CPL], (b * BODIES + q) * 16 + (16 if m else 32))
                    pe.wait_ge(maskA_made, c + 1)
                    turn(m % 2, m // CPL, m % CPL)
                products(c, k % 2, q * (BODY * CJ) + k * CJ)

            def attend(b, bodies):
                pe.wait_ge(acc_copied, b * 2 + 2)
                clear()
                with pe.Fori(0, bodies) as q:
                    for k in range(BODY):
                        chunk(b, q, k)

            clear().then_inc(masks_used, 2)
            pe.wait_ge(adj_loaded[0], 16)
            turn(0, 0, 0)
            with pe.Fori(0, BLOCKS - 1) as b:
                attend(b, BODIES)
            attend(BLOCKS - 1, BODIES - 1)
            for k in range(BODY):
                chunk(BLOCKS - 1, BODIES - 1, k, turn_next=k < BODY - 1)


_INS = ["x", "adj", "L0_gnn_W", "L0_gnn_a", "L0_gnn_gamma", "L0_gnn_beta"]


def kernel(**inputs):
    import numpy as _np
    import concourse.bacc as _bacc
    from concourse import mybir as _mybir
    from concourse.bass_utils import run_bass_kernel_spmd as _run

    nc = _bacc.Bacc("TRN2", target_bir_lowering=False, num_devices=1)
    arrays, args = {}, []
    for name in _INS:
        arr = _np.ascontiguousarray(inputs[name])
        arrays[f"in_{name}_dram"] = arr
        args.append(nc.dram_tensor(f"in_{name}_dram", arr.shape, _mybir.dt.from_np(arr.dtype), kind="ExternalInput").ap())
    o = nc.dram_tensor("out_0_dram", arrays["in_x_dram"].shape, _mybir.dt.float32, kind="ExternalOutput").ap()
    bass_gat_preln_kernel(nc, *args, o)
    r = _run(nc, [arrays], core_ids=[0])
    return r.results[0]["out_0_dram"]
```

```python
import math

import concourse.bass as bass
from concourse import mybir
from contextlib import ExitStack

RMAX = bass.bass_isa.ReduceOp.max


def bass_gat_preln_kernel(nc, x, adj, W, a, gamma, beta, out):
    fp32 = mybir.dt.float32
    bf16 = mybir.dt.bfloat16
    fp16 = mybir.dt.float16
    ALU = mybir.AluOpType
    ACT = mybir.ActivationFunctionType
    AX = mybir.AxisListType

    P = 128
    N, F = x.shape
    HD = a.shape[0] // 2
    H = W.shape[1] // HD
    HA = HD + 1
    NT = N // P
    EPS = 1e-5
    SLOPE = 0.2

    RANGE = 14.0
    H_LOW, H_HIGH = 2.0 ** -3, 2.0 ** 5

    PG = 8
    PSTEPS = NT // PG
    SG = 16
    SSTEPS = NT // SG

    IB = 4
    BI = IB * P
    BLOCKS = N // BI
    CJ = 2
    LJ = 4
    NBUF = 4
    CPL = LJ // CJ
    CHUNKS = NT // CJ
    LOADS = NT // LJ
    WC = 4 * HA
    SCALE = 10 * math.log(2.0)
    LO = 2048.0
    DEEP = 4
    ZH = H - 1

    ctx = ExitStack()
    with ctx:
        def sb(name, shape, dt):
            return ctx.enter_context(nc.sbuf_tensor(name, shape, dt))

        def sem(name):
            return ctx.enter_context(nc.semaphore(name))

        weights = sb("weights", [P, NT, H, WC], fp16)
        adj_in = sb("adj_in", [P, NBUF, IB, LJ * P], fp32)
        maskA = sb("maskA", [P, DEEP, CJ, BI], fp16)
        maskB = sb("maskB", [P, 2, H, CJ, BI], fp16)
        below = sb("below", [P, DEEP, ZH, CJ, BI], bf16)
        s_rows = sb("s_rows", [P, 2, H, BI], fp32)
        hbig = sb("hbig", [P, NT * H * HA], fp32)
        haug = hbig[:, :].rearrange("p (t h c) -> p t h c", h=H, c=HA)
        sd = sb("sd", [P, 2 * H, NT], fp32)
        negd = sb("negd", [P, NT, H], fp32)
        coefU = sb("coefU", [P, NT, H], fp32)
        coefV = sb("coefV", [P, NT, H], fp32)
        expU = sb("expU", [P, NT, H], fp32)
        expV = sb("expV", [P, NT, H], fp32)
        ident = sb("ident", [P, P], fp32)
        ident16 = sb("ident16", [P, P], bf16)
        ones = sb("ones", [P, P], fp32)
        zero16 = sb("zero16", [1, 512], fp16)
        gam = sb("gam", [P, F], fp32)
        bet = sb("bet", [P, F], fp32)
        small = sb("small", [P, 64], fp32)
        hsum = sb("hsum", [P, H * HA], fp32)

        zf = below[:, :, :, :, :].bitcast(fp32).rearrange("p a b c d -> p (a b c d)")
        bf = maskB[:, :, :, :, :].bitcast(fp32).rearrange("p a b c d -> p (a b c d)")
        wf = weights[:, :, :, :].bitcast(fp32).rearrange("p a b c -> p (a b c)")
        xin = wf[:, 0:NT * F].rearrange("p (t f) -> p t f", f=F)
        hn = wf[:, NT * F:2 * NT * F].rearrange("p (t f) -> p t f", f=F)
        place = [0]

        def take(n):
            place[0] += n
            assert place[0] <= zf.shape[1]
            return zf[:, place[0] - n:place[0]]

        hnT = take(2 * PG * P).rearrange("p (s t n) -> p s t n", s=2, n=P)
        Wsb = take(F)
        WT = take(F)
        WA = take(2 * H)
        Asd = take(2 * H)
        stats = take(NT * 6).rearrange("p (t c) -> p t c", c=6)
        mv = take(NT * 2).rearrange("p (t c) -> p t c", c=2)
        rstd = take(NT)
        nmr = take(NT)
        vpe = take(NT)
        epsc = sb("epsc", [P, SG], fp32)[:, :]
        mhalf = sb("mhalf", [P, SG], fp32)[:, :]
        mone = sb("mone", [P, IB * H], fp32)[:, :]
        inv_lo = sb("inv_lo", [P, 1], fp32)[:, :]
        WG = 4
        WSTEPS = NT // WG
        XN = WG * H * HA
        xw = [bf[:, k * XN:(k + 1) * XN].rearrange("p (t h c) -> p t h c", h=H, c=HA) for k in range(2)]
        sd_st = bf[:, 2 * XN:2 * XN + 4 * P].rearrange("p (k n) -> p k n", n=P)
        o = 2 * XN + 4 * P
        yv = bf[:, o:o + 2 * NT * H].rearrange("p (k h t) -> p k h t", h=H, k=2)
        o += 2 * NT * H
        hmax = bf[:, o:o + PSTEPS]

        LN_FLOATS = 6 * IB * F + 8 * IB

        def ln_buffers(region, at):
            def rows(k, n=1):
                return region[:, at + k * IB * F:at + (k + n) * IB * F]

            return {
                "feat": rows(0).rearrange("p (i f) -> p i f", f=F),
                "tree": rows(1).rearrange("p (i f) -> p i f", f=F),
                "sq": rows(2).rearrange("p (i f) -> p i f", f=F),
                "yout": rows(3).rearrange("p (i f) -> p i f", f=F),
                "x_res": rows(4, 2).rearrange("p (s i f) -> p s i f", s=2, f=F),
                "lnst": region[:, at + 6 * IB * F:at + 6 * IB * F + 8 * IB].rearrange("p (k i) -> p k i", i=IB),
            }

        e = 0
        acc_sb = hbig[:, 0:IB * H * WC].rearrange("p (i h c) -> p i h c", h=H, c=WC)
        e += IB * H * WC
        uu = hbig[:, e:e + IB * H * HA].rearrange("p (i h c) -> p i h c", h=H, c=HA)
        e += IB * H * HA
        vv = hbig[:, e:e + IB * H * HA].rearrange("p (i h c) -> p i h c", h=H, c=HA)
        e += IB * H * HA
        ln_fast = ln_buffers(hbig[:, :], e)
        e += LN_FLOATS
        feat, x_res = ln_fast["feat"], ln_fast["x_res"]
        e0 = hbig[:, e:e + IB * H].rearrange("p (i h) -> p i h", h=H)
        e += IB * H
        assert e <= NT * H * HA

        logits = wf[:, 0:N]
        probs = wf[:, N:2 * N]
        cap = adj_in[:, :, :, :].rearrange("p a b c -> p (a b c)")[:, 0:N]
        d_rows = s_rows[:, :, :, :].rearrange("p a b c -> p (a b c)")
        DC = N // 2
        ln_gen = ln_buffers(bf, 0)
        probsT = maskA[:, :, :, :].bitcast(fp32).rearrange("p s u i -> p s (u i)")
        TG = 4
        GROUPS = NT // TG
        neg_max = small[:, 38:39]
        denom = small[:, 39:40]
        inv_denom = small[:, 40:41]
        flag = sb("flag", [P, 1], mybir.dt.int32)

        bank = [ctx.enter_context(nc.psum_tensor(f"bank{i}", [P, 512], fp32)) for i in range(8)]
        ptr = [[bank[0], bank[1]], [bank[6], bank[7]]]
        ph = [bank[2], bank[3]]
        psd = bank[4]
        pmisc = bank[5]
        accA = [bank[i][:, 0:3 * WC].rearrange("p (h c) -> p h c", c=WC) for i in range(IB)]
        accB = [bank[4 + i][:, 0:2 * WC].rearrange("p (i c) -> p i c", c=WC) for i in range(IB // 2)]
        turned = [bank[6 + s][:, :].bitcast(bf16).rearrange("p (u i) -> p u i", i=BI) for s in range(2)]

        def acc(it, h):
            return accA[it][:, h, :] if h < 3 else accB[it // 2][:, it % 2, :]

        sd_dram = nc.dram_tensor("sd_scratch", [2 * H, N], fp32, kind="Internal").ap()

        consts_loaded = sem("consts_loaded")
        a_loaded = sem("a_loaded")
        consts_made = sem("consts_made")
        asd_clear = sem("asd_clear")
        wt_turned = sem("wt_turned")
        wt_copied = sem("wt_copied")
        wa_made = sem("wa_made")
        wa_copied = sem("wa_copied")
        x_loaded = [sem(f"x_loaded{i}") for i in range(SSTEPS)]
        stats_made = sem("stats_made")
        moments_made = sem("moments_made")
        norm_made = sem("norm_made")
        hn_made = sem("hn_made")
        hn_turned = sem("hn_turned")
        hnT_copied = sem("hnT_copied")
        h_made = sem("h_made")
        h_copied = sem("h_copied")
        hmax_made = sem("hmax_made")
        s_turned = sem("s_turned")
        s_copied = sem("s_copied")
        sd_stored = sem("sd_stored")
        col_max = sem("col_max")
        all_max = sem("all_max")
        bias_made = sem("bias_made")
        exps_made = sem("exps_made")
        expU_negated = sem("expU_negated")
        y_made = sem("y_made")
        coefs_made = sem("coefs_made")
        scaled = sem("scaled")
        hi_made = sem("hi_made")
        rest_made = sem("rest_made")
        lo_made = sem("lo_made")
        hsum_made = sem("hsum_made")
        hsum_copied = sem("hsum_copied")
        adj_loaded = [sem(f"adj_loaded{i}") for i in range(NBUF)]
        rows_loaded = [sem(f"rows_loaded{i}") for i in range(2)]
        tile_turned = sem("tile_turned")
        maskA_made = sem("maskA_made")
        below_made = sem("below_made")
        masks_made = sem("masks_made")
        masks_used = sem("masks_used")
        acc_copied = sem("acc_copied")
        acc_read = sem("acc_read")
        pool_step = sem("pool_step")
        dve_step = sem("dve_step")
        flag_made = sem("flag_made")
        gen_adj = sem("gen_adj")
        gen_d = sem("gen_d")
        gen_d_used = sem("gen_d_used")
        gen_logits = sem("gen_logits")
        gen_probs = sem("gen_probs")
        gen_turned = sem("gen_turned")
        gen_copied = sem("gen_copied")
        gen_multiplied = sem("gen_multiplied")
        gen_summed = sem("gen_summed")
        gen_feat = sem("gen_feat")
        y_stored = sem("y_stored")

        block = ctx.enter_context(nc.Block())

        def chain_on(eng, counter):
            count = [0]

            def step(ins):
                count[0] += 1
                ins.then_inc(counter, 1)
                eng.wait_ge(counter, count[0])
            return step

        def fast(eng):
            eng.wait_ge(flag_made, 1)
            return eng.value_load(flag[0:1, 0:1], min_val=0, max_val=1)

        @block.sync
        def _(sp):
            x_v = x.rearrange("(t p) f -> p t f", p=P)
            for g in range(SSTEPS):
                sp.dma_start(xin[:, g * SG:(g + 1) * SG], x_v[:, g * SG:(g + 1) * SG, :]).then_inc(x_loaded[g], 16)
            sp.dma_start(Wsb, W).then_inc(consts_loaded, 16)
            sp.dma_start(gam[:, :], gamma.partition_broadcast(P)).then_inc(consts_loaded, 16)
            sp.dma_start(bet[:, :], beta.partition_broadcast(P)).then_inc(consts_loaded, 16)
            sp.wait_ge(s_copied, 1)
            sp.dma_start(sd_dram.rearrange("(k h) (t p) -> (h t) k p", p=P, k=4), sd_st).then_inc(sd_stored, 16)
            sp.wait_ge(sd_stored, 16)
            adj_v = adj.rearrange("(b i p) j -> b p i j", i=IB, p=P)
            adj_t = adj.rearrange("(t p) j -> t p j", p=P)
            xr_v = x.rearrange("(b i p) f -> b p i f", i=IB, p=P)

            def block_loads(b, half):
                sp.wait_ge(acc_read, b + 1)
                sp.dma_start(s_rows[:, half], sd_dram[0:H, bass.ds(b * BI, BI)].partition_broadcast(P)).then_inc(rows_loaded[half], 16)
                sp.dma_start(x_res[:, half], xr_v[b]).then_inc(rows_loaded[half], 16)
                with sp.Fori(0, LOADS // NBUF) as q:
                    for k in range(NBUF):
                        sp.wait_ge(tile_turned, b * CHUNKS + q * (NBUF * CPL) + (k + 1) * CPL)
                        sp.dma_start(adj_in[:, k], adj_v[b][:, :, bass.ds(q * (NBUF * LJ * P) + k * LJ * P, LJ * P)]).then_inc(adj_loaded[k], 16)

            def general():
                sp.wait_ge(coefs_made, 1)
                sp.wait_ge(flag_made, 1)
                with sp.Fori(0, BLOCKS) as b:
                    sp.wait_ge(acc_read, b + 2)
                    sp.dma_start(ln_gen["x_res"][:, 0], xr_v[b]).then_inc(rows_loaded[0], 16)
                    with sp.Fori(0, IB) as i:
                        sp.wait_ge(gen_feat, (b * IB + i) * H + 1)
                        sp.dma_start(cap, adj_t[b * IB + i]).then_inc(gen_adj, 16)
                        with sp.Fori(0, H) as h:
                            for c in range(2):
                                sp.wait_ge(gen_d_used, ((b * IB + i) * H + h) * 2 + (c + 1))
                                sp.dma_start(d_rows, sd_dram[bass.ds(h + H, 1), c * DC:(c + 1) * DC].partition_broadcast(P)).then_inc(gen_d, 16)

            takes = fast(sp)
            with sp.If(takes > 0):
                sp.wait_ge(hsum_copied, 1)
                with sp.Fori(0, BLOCKS // 2) as bp:
                    for half in range(2):
                        block_loads(bp * 2 + half, half)
            with sp.Else():
                general()

        @block.gpsimd
        def _(pool):
            def chain():
                return chain_on(pool, pool_step)

            nc.gpsimd.memset(Asd, 0.0).then_inc(asd_clear, 1)
            nc.gpsimd.memset(ones[:, :], 1.0)
            nc.gpsimd.memset(zero16[:, :], 0.0)
            nc.gpsimd.memset(mhalf, -0.5)
            nc.gpsimd.memset(mone, -1.0)
            nc.gpsimd.memset(epsc, EPS)
            nc.gpsimd.memset(inv_lo, 1.0 / LO)
            nc.gpsimd.memset(haug[:, :, :, HD:HA], 1.0)
            nc.gpsimd.memset(ident[:, :], 0.0).then_inc(pool_step, 1)
            pool.wait_ge(pool_step, 1)
            nc.gpsimd.affine_select(out=ident[:, :], in_=ident[:, :], compare_op=ALU.not_equal, fill=1.0,
                                    base=0, pattern=[[-1, P]], channel_multiplier=1).then_inc(pool_step, 1)
            pool.wait_ge(pool_step, 2)
            pool.sem_clear(pool_step)
            nc.gpsimd.tensor_copy(ident16[:, :], ident[:, :]).then_inc(consts_made, 1)
            pool.wait_ge(asd_clear, 1)
            a_v = a.rearrange("(k d) o -> k d o", k=2)
            for h in range(H):
                for k in range(2):
                    pool.dma_start(Asd[h * HD:(h + 1) * HD, k * H + h:k * H + h + 1], a_v[k]).then_inc(a_loaded, 16)
            for g in range(SSTEPS):
                ts = slice(g * SG, (g + 1) * SG)
                pool.wait_ge(moments_made, g + 1)
                step = chain()
                step(nc.gpsimd.tensor_tensor(vpe[:, ts], mv[:, ts, 1], epsc, ALU.add))
                step(nc.gpsimd.tensor_tensor(rstd[:, ts], vpe[:, ts], mhalf, ALU.pow))
                step(nc.gpsimd.tensor_tensor(nmr[:, ts], mv[:, ts, 0], rstd[:, ts], ALU.mult))
                pool.sem_clear(pool_step)
                nc.gpsimd.tensor_scalar(nmr[:, ts], nmr[:, ts], -1.0, None, ALU.mult).then_inc(norm_made, 1)
            pool.wait_ge(col_max, 3)
            nc.gpsimd.partition_all_reduce(small[:, 16:16 + 2 * H + 1], small[:, 0:2 * H + 1], P, RMAX).then_inc(all_max, 1)

            pool.wait_ge(consts_loaded, 48)
            pool.sem_inc(acc_read, 2)
            out_v = out.rearrange("(b i p) f -> b p i f", i=IB, p=P)

            def over(ap, n):
                return ap.unsqueeze(len(ap.shape)).broadcast_to(list(ap.shape) + [n])

            def finish(b, half, buf, step):
                feat, tree, sq, yout, lnst = (buf[k] for k in ("feat", "tree", "sq", "yout", "lnst"))

                def tree_sum(src, dst):
                    w = F // 2
                    step(nc.gpsimd.tensor_tensor(tree[:, :, 0:w], src[:, :, 0:w], src[:, :, w:F], ALU.add))
                    while w > 2:
                        w //= 2
                        step(nc.gpsimd.tensor_tensor(tree[:, :, 0:w], tree[:, :, 0:w], tree[:, :, w:2 * w], ALU.add))
                    step(nc.gpsimd.tensor_tensor(dst, tree[:, :, 0], tree[:, :, 1], ALU.add))

                tree_sum(feat, lnst[:, 0])
                step(nc.gpsimd.tensor_scalar(lnst[:, 1], lnst[:, 0], 1.0 / F, None, ALU.mult))
                step(nc.gpsimd.tensor_tensor(feat, feat, over(lnst[:, 1], F), ALU.subtract))
                step(nc.gpsimd.tensor_tensor(sq, feat, feat, ALU.mult))
                tree_sum(sq, lnst[:, 2])
                step(nc.gpsimd.tensor_scalar(lnst[:, 3], lnst[:, 2], 1.0 / F, EPS, ALU.mult, ALU.add))
                step(nc.gpsimd.tensor_tensor(lnst[:, 4], lnst[:, 3], mhalf[:, 0:IB], ALU.pow))
                step(nc.gpsimd.tensor_tensor(feat, feat, over(lnst[:, 4], F), ALU.mult))
                step(nc.gpsimd.tensor_tensor(feat, feat, gam[:, :].unsqueeze(1).broadcast_to([P, IB, F]), ALU.mult))
                step(nc.gpsimd.tensor_tensor(feat, feat, bet[:, :].unsqueeze(1).broadcast_to([P, IB, F]), ALU.add))
                pool.sem_clear(pool_step)
                nc.gpsimd.tensor_tensor(yout, feat, buf["x_res"][:, half], ALU.add).then_inc(acc_read, 1)
                pool.wait_ge(acc_read, b + 3)
                pool.dma_start(out_v[b], yout).then_inc(y_stored, 16)
                pool.wait_ge(y_stored, b * 16 + 16)

            def combine(b, half):
                hs_b = hsum[:, :].rearrange("p (h c) -> p h c", c=HA).unsqueeze(1).broadcast_to([P, IB, H, HA])
                pool.wait_ge(acc_copied, b * 2 + 4)
                cu = over(coefU[:, bass.ds(b * IB, IB), :], HA)
                cv = over(coefV[:, bass.ds(b * IB, IB), :], HA)

                def part(k):
                    return acc_sb[:, :, :, k * HA:(k + 1) * HA]

                step = chain()
                nc.gpsimd.tensor_tensor(uu, part(1), inv_lo.unsqueeze(2).unsqueeze(3).broadcast_to([P, IB, H, HA]), ALU.mult)
                step(nc.gpsimd.tensor_scalar(vv, part(3), 1.0 / LO, None, ALU.mult))
                nc.gpsimd.tensor_tensor(uu, uu, part(0), ALU.add)
                step(nc.gpsimd.tensor_tensor(vv, vv, part(2), ALU.add))
                nc.gpsimd.tensor_tensor(uu, uu, cu, ALU.mult)
                step(nc.gpsimd.tensor_tensor(vv, vv, cv, ALU.mult))
                step(nc.gpsimd.tensor_tensor(uu, uu, vv, ALU.add))
                step(nc.gpsimd.tensor_scalar(e0, uu[:, :, :, HD], 0.0, None, ALU.is_equal))
                step(nc.gpsimd.tensor_tensor(vv, hs_b, over(e0, HA), ALU.mult))
                step(nc.gpsimd.tensor_tensor(uu, uu, vv, ALU.add))
                step(nc.gpsimd.tensor_tensor(e0, uu[:, :, :, HD], mone.rearrange("p (i h) -> p i h", h=H), ALU.pow))
                step(nc.gpsimd.tensor_tensor(feat.rearrange("p i (h c) -> p i h c", c=HD), uu[:, :, :, 0:HD],
                                             over(e0, HD), ALU.mult))
                return step

            takes = fast(pool)
            with pool.If(takes > 0):
                pool.wait_ge(hsum_copied, 1)
                pool.wait_ge(coefs_made, 1)
                with pool.Fori(0, BLOCKS // 2) as bp:
                    for half in range(2):
                        pool.wait_ge(rows_loaded[half], bp * 32 + 32)
                        step = combine(bp * 2 + half, half)
                        finish(bp * 2 + half, half, ln_fast, step)
            with pool.Else():
                with pool.Fori(0, BLOCKS) as b:
                    pool.wait_ge(gen_feat, b * (IB * H) + (IB * H + 1))
                    pool.wait_ge(rows_loaded[0], b * 16 + 16)
                    finish(b, 0, ln_gen, chain())

        @block.vector
        def _(dve):
            dve.sem_inc(lo_made, 2)
            dve.sem_inc(masks_made, DEEP)
            dve.sem_inc(maskA_made, 1)

            for g in range(SSTEPS):
                dve.wait_ge(x_loaded[g], 16)
                for t in range(g * SG, (g + 1) * SG):
                    last = nc.vector.bn_stats(stats[:, t], xin[:, t])
                last.then_inc(stats_made, 1)
                dve.wait_ge(stats_made, g + 1)
                for t in range(g * SG, (g + 1) * SG):
                    last = nc.vector.bn_aggr(mv[:, t], stats[:, t])
                last.then_inc(moments_made, 1)

            dve.wait_ge(wt_turned, 1)
            nc.vector.tensor_copy(WT, pmisc[:, 0:F]).then_inc(wt_copied, 1)
            dve.wait_ge(wa_made, 1)
            nc.vector.tensor_copy(WA, pmisc[:, F:F + 2 * H]).then_inc(wa_copied, 1)

            def max_h(st):
                dve.wait_ge(h_copied, st + 1)
                nc.vector.tensor_reduce(hmax[:, st:st + 1], haug[:, st * PG:(st + 1) * PG, :, 0:HD], axis=AX.XYZ, op=ALU.max,
                                        apply_absolute_value=True).then_inc(hmax_made, 1)

            LAG = 2
            for st in range(PSTEPS + LAG):
                if st < PSTEPS:
                    dve.wait_ge(hn_turned, st + 1)
                    if st >= 2:
                        dve.wait_ge(h_made, st - 1)
                    for i in range(2):
                        last = nc.vector.tensor_copy(hnT[:, st % 2, 4 * i:4 * i + 4],
                                                     ptr[st % 2][i][:, :].rearrange("p (t n) -> p t n", n=P))
                    last.then_inc(hnT_copied, 1)
                if st >= LAG:
                    max_h(st - LAG)

            dve.wait_ge(h_copied, PSTEPS)
            dve.wait_ge(hmax_made, PSTEPS)
            nc.vector.tensor_reduce(small[:, 0:H], sd[:, H:2 * H, :], axis=AX.X, op=ALU.max).then_inc(col_max, 1)
            nc.vector.tensor_reduce(small[:, H:2 * H], sd[:, H:2 * H, :], axis=AX.X, op=ALU.min, negate=True).then_inc(col_max, 1)
            nc.vector.tensor_reduce(small[:, 2 * H:2 * H + 1], hmax, axis=AX.X, op=ALU.max).then_inc(col_max, 1)
            dve.wait_ge(s_turned, 1)
            nc.vector.tensor_copy(sd_st, pmisc[:, 0:4 * P].rearrange("p (k n) -> p k n", n=P)).then_inc(s_copied, 1)
            nc.vector.tensor_scalar(negd[:, :, :].rearrange("p t h -> p h t"), sd[:, H:2 * H, :], -1.0, None, ALU.mult)
            dve.wait_ge(all_max, 1)
            nc.vector.tensor_scalar(small[:, 56:60], small[:, 16:16 + H], -1.0, SCALE, ALU.mult, ALU.add)
            nc.vector.tensor_scalar(small[:, 60:64], small[:, 16:16 + H], -SLOPE, SCALE, ALU.mult, ALU.add).then_inc(bias_made, 1)
            for h in range(H):
                nc.vector.tensor_scalar(yv[:, 0, h], sd[:, h, :], small[:, 16 + h:17 + h], 0.0, ALU.add, ALU.min)
                last = nc.vector.tensor_scalar(yv[:, 1, h], sd[:, h, :], small[:, 16 + h:17 + h], 0.0, ALU.add, ALU.max)
            last.then_inc(y_made, 1)
            step = chain_on(dve, dve_step)
            nc.vector.tensor_scalar(small[:, 36:37], small[:, 24:25], H_HIGH, None, ALU.is_le)
            nc.vector.tensor_scalar(small[:, 37:38], small[:, 24:25], H_LOW, None, ALU.is_ge)
            step(nc.vector.tensor_tensor(small[:, 32:36], small[:, 16:16 + H], small[:, 16 + H:16 + 2 * H], ALU.add))
            step(nc.vector.tensor_scalar(small[:, 32:36], small[:, 32:36], RANGE, None, ALU.is_le))
            step(nc.vector.tensor_reduce(small[:, 41:42], small[:, 32:38], axis=AX.X, op=ALU.min))
            nc.vector.tensor_copy(flag[:, :], small[:, 41:42]).then_inc(flag_made, 1)
            dve.sem_clear(dve_step)
            def general():
                dve.wait_ge(coefs_made, 1)
                dve.wait_ge(sd_stored, 16)
                dve.sem_inc(gen_d_used, 1)
                dve.sem_inc(gen_feat, 1)
                BIG = 9e15
                with dve.Fori(0, BLOCKS) as b:
                    with dve.Fori(0, IB) as i:
                        t = b * IB + i
                        dve.wait_ge(acc_read, b + 2)
                        dve.wait_ge(gen_adj, t * 16 + 16)
                        step = chain_on(dve, dve_step)
                        step(nc.vector.tensor_scalar(cap, cap, 0.0, 2 * BIG, ALU.is_gt, ALU.mult))
                        step(nc.vector.tensor_scalar(cap, cap, -BIG, None, ALU.add))
                        dve.sem_clear(dve_step)
                        with dve.Fori(0, H) as h:
                            m = t * H + h
                            step = chain_on(dve, dve_step)
                            for c in range(2):
                                part = logits[:, c * DC:(c + 1) * DC]
                                dve.wait_ge(gen_d, m * 32 + (c + 1) * 16)
                                nc.vector.tensor_scalar(part, d_rows, sd[:, bass.ds(h, 1), bass.ds(t, 1)].squeeze(2), None,
                                                        ALU.add).then_inc(gen_d_used, 1)
                                dve.wait_ge(gen_d_used, m * 2 + (c + 2))
                                step(nc.vector.scalar_tensor_tensor(part, part, SLOPE, part, ALU.mult, ALU.max))
                                step(nc.vector.tensor_tensor(part, part, cap[:, c * DC:(c + 1) * DC], ALU.min))
                            nc.vector.tensor_reduce(neg_max, logits, axis=AX.X, op=ALU.max, negate=True).then_inc(gen_logits, 1)
                            dve.sem_clear(dve_step)
                            for g in range(GROUPS):
                                dve.wait_ge(gen_turned, m * GROUPS + (g + 1))
                                if g >= 2:
                                    dve.wait_ge(gen_multiplied, m * GROUPS + (g - 1))
                                nc.vector.tensor_copy(probsT[:, g % 2], bank[6 + g % 2][:, :]).then_inc(gen_copied, 1)
                            dve.wait_ge(gen_summed, m + 1)
                            step = chain_on(dve, dve_step)
                            step(nc.vector.reciprocal(inv_denom, denom))
                            dve.sem_clear(dve_step)
                            nc.vector.tensor_scalar(ln_gen["feat"][:, bass.ds(i, 1), bass.ds(h * HD, HD)].squeeze(1), bank[0][:, 0:HD],
                                                    inv_denom, None, ALU.mult).then_inc(gen_feat, 1)

            takes = fast(dve)
            with dve.If(takes > 0):
                dve.wait_ge(exps_made, 1)
                nc.vector.tensor_scalar(expU[:, :, :], expU[:, :, :], -1.0, None, ALU.mult).then_inc(expU_negated, 1)
                dve.wait_ge(expU_negated, 1)

                with dve.Fori(0, WSTEPS) as g:
                    for k, ex in enumerate((expU, expV)):
                        dve.wait_ge(lo_made, g * 2 + (k + 1))
                        nc.vector.tensor_tensor(xw[k], haug[:, bass.ds(g * WG, WG)],
                                                ex[:, bass.ds(g * WG, WG), :].unsqueeze(3).broadcast_to([P, WG, H, HA]),
                                                ALU.mult).then_inc(scaled, 1)
                    for k in range(2):
                        dve.wait_ge(hi_made, g * 2 + (k + 1))
                        nc.vector.tensor_tensor(xw[k], xw[k], weights[:, bass.ds(g * WG, WG), :, 2 * k * HA:(2 * k + 1) * HA],
                                                ALU.subtract).then_inc(rest_made, 1)
                dve.wait_ge(hsum_made, 1)
                nc.vector.tensor_copy(hsum[:, :], pmisc[:, 0:H * HA]).then_inc(hsum_copied, 1)

                dve.wait_ge(lo_made, 2 * WSTEPS + 2)
                dve.wait_ge(coefs_made, 1)
                dve.wait_ge(sd_stored, 16)

                def edges(c, k):
                    dve.wait_ge(tile_turned, c + (2 * NBUF + 1))
                    dve.wait_ge(masks_used, c + 1)
                    nc.vector.tensor_scalar(maskA[:, k % DEEP], turned[k % 2], 0.0, 1.0, ALU.is_le, ALU.subtract).then_inc(maskA_made, 1)

                def masks(c, k, half, next_edges=True):
                    dve.wait_ge(masks_used, c + (DEEP - 1))
                    dve.wait_ge(maskA_made, c + 2)
                    for u in range(CJ):
                        jt = k * CJ + u
                        nc.vector.scalar_tensor_tensor(maskB[:, k % 2, 0, u], s_rows[:, half, 0], negd[:, jt:jt + 1, 0],
                                                       maskA[:, k % DEEP, u], ALU.is_lt, ALU.logical_and)
                    if next_edges:
                        edges(c + 1, k + 1)
                    dve.wait_ge(below_made, c + 1)
                    nc.vector.tensor_tensor(maskB[:, k % 2, H - ZH:H].rearrange("p h u i -> p h (u i)"),
                                            below[:, k % DEEP].rearrange("p h u i -> p h (u i)"),
                                            maskA[:, k % DEEP].rearrange("p u i -> p (u i)").unsqueeze(1).broadcast_to([P, ZH, CJ * BI]),
                                            ALU.logical_and).then_inc(masks_made, 1)

                def flush(b):
                    dve.wait_ge(masks_used, b * CHUNKS + DEEP)
                    dve.wait_ge(acc_read, b + 1)
                    nc.vector.tensor_copy(acc_sb[:, 2, 0:3], accA[2])
                    nc.vector.tensor_copy(acc_sb[:, 3, 0:3], accA[3])
                    nc.vector.tensor_copy(acc_sb[:, 0:2, 3], accB[0]).then_inc(acc_copied, 1)

                def attend(b, half, loads, last=False):
                    dve.wait_ge(rows_loaded[half], loads)
                    for k in range(CHUNKS):
                        masks(b * CHUNKS + k, k, half, next_edges=not (last and k == CHUNKS - 1))
                        if k == 0:
                            flush(b)

                edges(0, 0)
                with dve.Fori(0, BLOCKS // 2 - 1) as bp:
                    for half in range(2):
                        attend(bp * 2 + half, half, bp * 32 + 32)
                for half in range(2):
                    attend(BLOCKS - 2 + half, half, 16 * BLOCKS, last=half == 1)
                flush(BLOCKS)
            with dve.Else():
                general()

        @block.scalar
        def _(act):
            LAG = 2
            for st in range(PSTEPS + LAG):
                if st < PSTEPS:
                    act.wait_ge(norm_made, st * PG // SG + 1)
                    for t in range(st * PG, (st + 1) * PG):
                        last = nc.scalar.activation(hn[:, t], xin[:, t], ACT.Relu, bias=nmr[:, t:t + 1], scale=rstd[:, t:t + 1])
                    last.then_inc(hn_made, 1)
                if st >= LAG:
                    t0 = (st - LAG) * PG
                    act.wait_ge(h_made, st - LAG + 1)
                    for i in range(2):
                        nc.scalar.activation(haug[:, t0 + 4 * i:t0 + 4 * i + 4, :, 0:HD],
                                             ph[i][:, :].rearrange("p (t h c) -> p t h c", h=H, c=HD), ACT.Copy)
                    nc.scalar.activation(sd[:, :, t0:t0 + PG], psd[:, 0:PG * 2 * H].rearrange("p (t c) -> p c t", c=2 * H),
                                         ACT.Copy).then_inc(h_copied, 1)

            act.wait_ge(bias_made, 1)
            for h in range(H):
                nc.scalar.activation(expU[:, :, h], sd[:, H + h, :], ACT.Exp, bias=small[:, 56 + h:57 + h])
                last = nc.scalar.activation(expV[:, :, h], sd[:, H + h, :], ACT.Exp, bias=small[:, 60 + h:61 + h], scale=SLOPE)
            last.then_inc(exps_made, 1)
            act.wait_ge(y_made, 1)
            nc.scalar.activation(coefU[:, :, :].rearrange("p t h -> p h t"), yv[:, 0], ACT.Exp, scale=1.0 - SLOPE)
            nc.scalar.activation(coefV[:, :, :].rearrange("p t h -> p h t"), yv[:, 1], ACT.Exp, scale=SLOPE - 1.0).then_inc(coefs_made, 1)
            def general():
                with act.Fori(0, NT * H) as m:
                    act.wait_ge(gen_logits, m + 1)
                    nc.scalar.activation(probs, logits, ACT.Exp, bias=neg_max, accum_out=denom).then_inc(gen_probs, 1)

            takes = fast(act)
            with act.If(takes > 0):
                with act.Fori(0, WSTEPS) as g:
                    for k in range(2):
                        act.wait_ge(scaled, g * 2 + (k + 1))
                        nc.scalar.activation(weights[:, bass.ds(g * WG, WG), :, 2 * k * HA:(2 * k + 1) * HA], xw[k],
                                             ACT.Copy).then_inc(hi_made, 1)
                    for k in range(2):
                        act.wait_ge(rest_made, g * 2 + (k + 1))
                        nc.scalar.activation(weights[:, bass.ds(g * WG, WG), :, (2 * k + 1) * HA:(2 * k + 2) * HA], xw[k],
                                             ACT.Copy, scale=LO).then_inc(lo_made, 1)

                def compare(c, k, half):
                    act.wait_ge(masks_made, c + 1)
                    for u in range(CJ):
                        for z in range(ZH):
                            h = H - ZH + z
                            last = nc.scalar.activation(below[:, k % DEEP, z, u], s_rows[:, half, h], ACT.Relu,
                                                        bias=negd[:, k * CJ + u:k * CJ + u + 1, h], scale=-1.0)
                    last.then_inc(below_made, 1)

                def flush(b):
                    act.wait_ge(masks_used, b * CHUNKS + DEEP)
                    act.wait_ge(acc_read, b + 1)
                    nc.scalar.activation(acc_sb[:, 0, 0:3], accA[0], ACT.Copy)
                    nc.scalar.activation(acc_sb[:, 1, 0:3], accA[1], ACT.Copy)
                    nc.scalar.activation(acc_sb[:, 2:4, 3], accB[1], ACT.Copy).then_inc(acc_copied, 1)

                act.wait_ge(hsum_copied, 1)
                with act.Fori(0, BLOCKS // 2) as bp:
                    for half in range(2):
                        b = bp * 2 + half
                        act.wait_ge(rows_loaded[half], bp * 32 + 32)
                        for k in range(CHUNKS):
                            compare(b * CHUNKS + k, k, half)
                            if k == 1:
                                flush(b)
                flush(BLOCKS)
            with act.Else():
                general()

        @block.tensor
        def _(pe):
            pe.sem_inc(tile_turned, 2 * NBUF)
            pe.wait_ge(consts_made, 1)
            pe.wait_ge(consts_loaded, 48)
            nc.tensor.transpose(pmisc[:, 0:F], Wsb, ident[:, :]).then_inc(wt_turned, 1)
            pe.wait_ge(wt_copied, 1)
            pe.wait_ge(a_loaded, 16 * 2 * H)
            nc.tensor.matmul(pmisc[:, F:F + 2 * H], WT, Asd, start=True, stop=True).then_inc(wa_made, 1)
            pe.wait_ge(wa_copied, 1)

            def turn_rows(st):
                pe.wait_ge(hn_made, st + 1)
                if st >= 2:
                    pe.wait_ge(hnT_copied, st - 1)
                for t in range(PG):
                    last = nc.tensor.transpose(ptr[st % 2][t // 4][:, (t % 4) * P:(t % 4 + 1) * P], hn[:, st * PG + t], ident[:, :])
                last.then_inc(hn_turned, 1)

            turn_rows(0)
            for st in range(PSTEPS):
                if st + 1 < PSTEPS:
                    turn_rows(st + 1)
                pe.wait_ge(hnT_copied, st + 1)
                if st >= 1:
                    pe.wait_ge(h_copied, st)
                for t in range(PG):
                    nc.tensor.matmul(ph[t // 4][:, (t % 4) * F:(t % 4 + 1) * F], hnT[:, st % 2, t], Wsb, start=True, stop=True)
                    last = nc.tensor.matmul(psd[:, t * 2 * H:(t + 1) * 2 * H], hnT[:, st % 2, t], WA, start=True, stop=True)
                last.then_inc(h_made, 1)
            pe.wait_ge(h_copied, PSTEPS)
            for k in range(4):
                last = nc.tensor.transpose(pmisc[:, k * P:(k + 1) * P], sd[:, 2 * k:2 * k + 2, :].rearrange("p h t -> p (h t)"), ident[:, :])
            last.then_inc(s_turned, 1)
            def general():
                with pe.Fori(0, BLOCKS * IB) as t:
                    with pe.Fori(0, H) as h:
                        m = t * H + h
                        pe.wait_ge(gen_probs, m + 1)

                        def turn_probs(g):
                            if g >= 2:
                                pe.wait_ge(gen_copied, m * GROUPS + (g - 1))
                            for u in range(TG):
                                j = (g * TG + u) * P
                                last = nc.tensor.transpose(bank[6 + g % 2][:, u * P:(u + 1) * P], probs[:, j:j + P], ident[:, :])
                            last.then_inc(gen_turned, 1)

                        turn_probs(0)
                        for g in range(GROUPS):
                            if g + 1 < GROUPS:
                                turn_probs(g + 1)
                            pe.wait_ge(gen_copied, m * GROUPS + (g + 1))
                            for u in range(TG):
                                last = nc.tensor.matmul(bank[0][:, 0:HD], probsT[:, g % 2, u * P:(u + 1) * P],
                                                        haug[:, g * TG + u, bass.ds(h, 1), 0:HD].squeeze(1),
                                                        start=g + u == 0, stop=g * TG + u == NT - 1)
                            last.then_inc(gen_multiplied, 1)
                        pe.drain().then_inc(gen_summed, 1)

            takes = fast(pe)
            with pe.If(takes > 0):
                pe.wait_ge(s_copied, 1)
                for t in range(NT):
                    last = nc.tensor.matmul(pmisc[:, 0:H * HA], ones[:, :], hbig[:, t * H * HA:(t + 1) * H * HA],
                                            start=t == 0, stop=t == NT - 1)
                last.then_inc(hsum_made, 1)
                pe.wait_ge(hsum_copied, 1)

                def turn(slot, k, cc):
                    a16 = adj_in[:, k].bitcast(bf16)
                    for u in range(CJ):
                        for it in range(IB):
                            j0 = 2 * (cc * CJ + u) * P
                            last = nc.tensor.transpose(turned[slot][:, u, it * P:(it + 1) * P],
                                                       a16[:, it, j0 + 1:j0 + 2 * P:2], ident16[:, :])
                    last.then_inc(tile_turned, 1)

                def clear():
                    for i in range(6):
                        last = nc.tensor.matmul(bank[i][:, :], zero16[0:1, 0:P], zero16[0:1, :], start=True, stop=False,
                                                skip_group_check=True)
                    return last

                def products(c, k):
                    pe.wait_ge(masks_made, c + (DEEP + 1))
                    for u in range(CJ):
                        w = weights[:, k * CJ + u]
                        for it in range(IB):
                            cols = slice(it * P, (it + 1) * P)
                            mA = maskA[:, k % DEEP, u, cols]
                            nc.tensor.matmul(accA[it][:, :, 0:2 * HA], mA, w[:, 0:3, 0:2 * HA], start=False, stop=False,
                                             skip_group_check=True)
                            nc.tensor.matmul(accB[it // 2][:, it % 2, 0:2 * HA], mA, w[:, 3, 0:2 * HA], start=False, stop=False,
                                             skip_group_check=True)
                            for h in range(H):
                                last = nc.tensor.matmul(acc(it, h), maskB[:, k % 2, h, u, cols], w[:, h], start=False, stop=False,
                                                        skip_group_check=True)
                    last.then_inc(masks_used, 1)

                def attend(b, last=False):
                    pe.wait_ge(acc_copied, b * 2 + 2)
                    clear()
                    for k in range(CHUNKS):
                        ahead = k + 2
                        load, part = divmod(ahead, CPL)
                        if not (last and ahead >= CHUNKS):
                            if part == 0:
                                pe.wait_ge(adj_loaded[load % NBUF], b * (16 * LOADS // NBUF) + 16 * (load // NBUF + 1))
                            pe.wait_ge(maskA_made, b * CHUNKS + (k + 2))
                            turn(ahead % 2, load % NBUF, part)
                        products(b * CHUNKS + k, k)

                clear().then_inc(masks_used, DEEP)
                pe.wait_ge(adj_loaded[0], 16)
                turn(0, 0, 0)
                turn(1, 0, 1)
                with pe.Fori(0, BLOCKS - 1) as b:
                    attend(b)
                attend(BLOCKS - 1, last=True)
            with pe.Else():
                general()


_INS = ["x", "adj", "L0_gnn_W", "L0_gnn_a", "L0_gnn_gamma", "L0_gnn_beta"]


def kernel(**inputs):
    import numpy as _np
    import concourse.bacc as _bacc
    from concourse import mybir as _mybir
    from concourse.bass_utils import run_bass_kernel_spmd as _run

    nc = _bacc.Bacc("TRN2", target_bir_lowering=False, num_devices=1)
    arrays, args = {}, []
    for name in _INS:
        arr = _np.ascontiguousarray(inputs[name])
        arrays[f"in_{name}_dram"] = arr
        args.append(nc.dram_tensor(f"in_{name}_dram", arr.shape, _mybir.dt.from_np(arr.dtype), kind="ExternalInput").ap())
    o = nc.dram_tensor("out_0_dram", arrays["in_x_dram"].shape, _mybir.dt.float32, kind="ExternalOutput").ap()
    bass_gat_preln_kernel(nc, *args, o)
    r = _run(nc, [arrays], core_ids=[0])
    return r.results[0]["out_0_dram"]
```

```python
import math

import concourse.bass as bass
from concourse import mybir
from contextlib import ExitStack

RMAX = bass.bass_isa.ReduceOp.max


def bass_gat_preln_kernel(nc, x, adj, W, a, gamma, beta, out):
    fp32 = mybir.dt.float32
    bf16 = mybir.dt.bfloat16
    fp16 = mybir.dt.float16
    ALU = mybir.AluOpType
    ACT = mybir.ActivationFunctionType
    AX = mybir.AxisListType

    P = 128
    N, F = x.shape
    HD = a.shape[0] // 2
    H = W.shape[1] // HD
    HA = HD + 1
    NT = N // P
    EPS = 1e-5
    SLOPE = 0.2

    RANGE = 14.0
    H_LOW, H_HIGH = 2.0 ** -3, 2.0 ** 5

    PG = 8
    PSTEPS = NT // PG
    AHEAD = 3
    SG = 8
    SSTEPS = NT // SG

    IB = 4
    BI = IB * P
    BLOCKS = N // BI
    CJ = 2
    LJ = 4
    NBUF = 4
    CPL = LJ // CJ
    CHUNKS = NT // CJ
    LOADS = NT // LJ
    WC = 4 * HA
    LO = 2048.0
    SCALE = 21 * math.log(2.0)
    DEEP = 4
    STATS_AT = 8
    FLUSH_AT = 2
    ZH = H - 1

    ctx = ExitStack()
    with ctx:
        def sb(name, shape, dt):
            return ctx.enter_context(nc.sbuf_tensor(name, shape, dt))

        def sem(name):
            return ctx.enter_context(nc.semaphore(name))

        weights = sb("weights", [P, NT, H, WC], fp16)
        adj_in = sb("adj_in", [P, NBUF, IB, LJ * P], fp32)
        maskA = sb("maskA", [P, DEEP, CJ, BI], fp16)
        maskB = sb("maskB", [P, 2, H, CJ, BI], fp16)
        below = sb("below", [P, DEEP, ZH, CJ, BI], bf16)
        s_rows = sb("s_rows", [P, 2, H, BI], fp32)
        hbig = sb("hbig", [P, NT * H * HA], fp32)
        haug = hbig[:, :].rearrange("p (t h c) -> p t h c", h=H, c=HA)
        sd = sb("sd", [P, 2 * H, NT], fp32)
        negd = sb("negd", [P, NT, H], fp32)
        coefs = sb("coefs", [P, NT, H, 2], fp32)
        expU = sb("expU", [P, NT, H], fp32)
        expV = sb("expV", [P, NT, H], fp32)
        ident = sb("ident", [P, P], fp32)
        ident16 = sb("ident16", [P, P], bf16)
        ones = sb("ones", [P, P], fp32)
        zero16 = sb("zero16", [1, 512], fp16)
        gam = sb("gam", [P, F], fp32)
        bet = sb("bet", [P, F], fp32)
        small = sb("small", [P, 64], fp32)
        hsum = sb("hsum", [P, H * HA], fp32)

        zf = below[:, :, :, :, :].bitcast(fp32).rearrange("p a b c d -> p (a b c d)")
        bf = maskB[:, :, :, :, :].bitcast(fp32).rearrange("p a b c d -> p (a b c d)")
        wf = weights[:, :, :, :].bitcast(fp32).rearrange("p a b c -> p (a b c)")
        xin = wf[:, 0:NT * F].rearrange("p (t f) -> p t f", f=F)
        hn = wf[:, NT * F:2 * NT * F].rearrange("p (t f) -> p t f", f=F)
        place = [0]

        def take(n):
            place[0] += n
            assert place[0] <= zf.shape[1]
            return zf[:, place[0] - n:place[0]]

        hnT = take(2 * PG * P).rearrange("p (s t n) -> p s t n", s=2, n=P)
        Wsb = take(F)
        WT = take(F)
        WA = take(2 * H)
        Asd = take(2 * H)
        stats = take(NT * 6).rearrange("p (t c) -> p t c", c=6)
        mv = take(NT * 2).rearrange("p (t c) -> p t c", c=2)
        rstd = take(NT)
        nmr = take(NT)
        vpe = take(NT)
        epsc = sb("epsc", [P, SG], fp32)[:, :]
        mhalf = sb("mhalf", [P, SG], fp32)[:, :]
        mone = sb("mone", [P, IB * H], fp32)[:, :]
        WG = 4
        WSTEPS = NT // WG
        XN = WG * H * HA
        XW = 4
        xw = [bf[:, k * XN:(k + 1) * XN].rearrange("p (t h c) -> p t h c", h=H, c=HA) for k in range(XW)]
        sd_st = bf[:, XW * XN:XW * XN + 4 * P].rearrange("p (k n) -> p k n", n=P)
        o = XW * XN + 4 * P
        yv = bf[:, o:o + 2 * NT * H].rearrange("p (k h t) -> p k h t", h=H, k=2)
        o += 2 * NT * H
        hmax = bf[:, o:o + PSTEPS]

        LN_FLOATS = 4 * IB * F + 10 * IB

        def ln_buffers(region, at):
            def rows(k, n=1):
                return region[:, at + k * IB * F:at + (k + n) * IB * F]

            st = at + 4 * IB * F
            return {
                "feat": rows(0).rearrange("p (i f) -> p i f", f=F),
                "yout": rows(1).rearrange("p (i f) -> p i f", f=F),
                "x_res": rows(2, 2).rearrange("p (s i f) -> p s i f", s=2, f=F),
                "stats": region[:, st:st + 6 * IB].rearrange("p (i c) -> p i c", c=6),
                "mv": region[:, st + 6 * IB:st + 8 * IB].rearrange("p (i c) -> p i c", c=2),
                "lnst": region[:, st + 8 * IB:st + 10 * IB].rearrange("p (k i) -> p k i", i=IB),
            }

        e = 0
        sums = hbig[:, 0:IB * H * 2 * HA].rearrange("p (i h k c) -> p i h k c", h=H, k=2, c=HA)
        e += IB * H * 2 * HA
        lows = hbig[:, e:e + IB * H * 2 * HA].rearrange("p (i h k c) -> p i h k c", h=H, k=2, c=HA)
        e += IB * H * 2 * HA
        uu = hbig[:, e:e + IB * H * HA].rearrange("p (i h c) -> p i h c", h=H, c=HA)
        e += IB * H * HA
        vv = hbig[:, e:e + IB * H * HA].rearrange("p (i h c) -> p i h c", h=H, c=HA)
        e += IB * H * HA
        ln_fast = ln_buffers(hbig[:, :], e)
        e += LN_FLOATS
        feat, x_res = ln_fast["feat"], ln_fast["x_res"]
        e0 = hbig[:, e:e + IB * H].rearrange("p (i h) -> p i h", h=H)
        e += IB * H
        assert e <= NT * H * HA

        logits = wf[:, 0:N]
        probs = wf[:, N:2 * N]
        cap = adj_in[:, :, :, :].rearrange("p a b c -> p (a b c)")[:, 0:N]
        d_rows = s_rows[:, :, :, :].rearrange("p a b c -> p (a b c)")
        DC = N // 2
        ln_gen = ln_buffers(bf, 0)
        probsT = maskA[:, :, :, :].bitcast(fp32).rearrange("p s u i -> p s (u i)")
        TG = 4
        GROUPS = NT // TG
        neg_max = small[:, 38:39]
        denom = small[:, 39:40]
        inv_denom = small[:, 40:41]
        flag = sb("flag", [P, 1], mybir.dt.int32)

        psum = ctx.enter_context(nc.psum_tensor("psum", [P, 8, 512], fp32))
        bank = [psum[:, i] for i in range(8)]
        ptr = [[bank[0], bank[1]], [bank[6], bank[7]]]
        ph = [bank[2], bank[3]]
        psd = bank[4]
        pmisc = bank[5]
        accA = [bank[i][:, 0:3 * WC].rearrange("p (h c) -> p h c", c=WC) for i in range(IB)]
        accB = [bank[4 + i][:, 0:2 * WC].rearrange("p (i c) -> p i c", c=WC) for i in range(IB // 2)]
        turned = [bank[6 + s][:, :].bitcast(bf16).rearrange("p (u i) -> p u i", i=BI) for s in range(2)]

        def copies(dst, z, q):
            yield (dst[:, 2 * q:2 * q + 2, 0:3].rearrange("p i h k c -> p i (h k) c"),
                   psum[:, 2 * q:2 * q + 2, 0:3 * WC].rearrange("p i (g z c) -> p i g z c", z=2, c=HA)[:, :, :, z])
            yield (dst[:, 2 * q:2 * q + 2, 3],
                   psum[:, 4 + q, 0:2 * WC].rearrange("p (i k z c) -> p i k z c", k=2, z=2, c=HA)[:, :, :, z])

        def acc(it, h):
            return accA[it][:, h, :] if h < 3 else accB[it // 2][:, it % 2, :]

        sd_dram = nc.dram_tensor("sd_scratch", [2 * H, N], fp32, kind="Internal").ap()

        w_loaded = sem("w_loaded")
        consts_loaded = sem("consts_loaded")
        a_loaded = sem("a_loaded")
        consts_made = sem("consts_made")
        asd_clear = sem("asd_clear")
        ones_made = sem("ones_made")
        wt_turned = sem("wt_turned")
        wt_copied = sem("wt_copied")
        wa_made = sem("wa_made")
        wa_copied = sem("wa_copied")
        x_loaded = [sem(f"x_loaded{i}") for i in range(SSTEPS)]
        stats_made = sem("stats_made")
        moments_made = sem("moments_made")
        norm_made = sem("norm_made")
        hn_made = sem("hn_made")
        hn_turned = sem("hn_turned")
        hnT_copied = sem("hnT_copied")
        h_made = sem("h_made")
        h_copied = sem("h_copied")
        hmax_made = sem("hmax_made")
        s_turned = sem("s_turned")
        s_copied = sem("s_copied")
        sd_stored = sem("sd_stored")
        col_max = sem("col_max")
        all_max = sem("all_max")
        bias_made = sem("bias_made")
        exps_made = sem("exps_made")
        expU_negated = sem("expU_negated")
        y_made = sem("y_made")
        coefs_made = sem("coefs_made")
        scaled = sem("scaled")
        hi_made = sem("hi_made")
        lo_made = sem("lo_made")
        hsum_made = sem("hsum_made")
        hsum_copied = sem("hsum_copied")
        adj_loaded = [sem(f"adj_loaded{i}") for i in range(NBUF)]
        rows_loaded = [sem(f"rows_loaded{i}") for i in range(2)]
        x_res_loaded = [sem(f"x_res_loaded{i}") for i in range(2)]
        tile_turned = sem("tile_turned")
        maskA_made = sem("maskA_made")
        below_made = sem("below_made")
        masks_made = sem("masks_made")
        masks_used = sem("masks_used")
        acc_copied = sem("acc_copied")
        acc_read = sem("acc_read")
        pool_step = sem("pool_step")
        dve_step = sem("dve_step")
        flag_made = sem("flag_made")
        gen_adj = sem("gen_adj")
        gen_d = sem("gen_d")
        gen_d_used = sem("gen_d_used")
        gen_logits = sem("gen_logits")
        gen_probs = sem("gen_probs")
        gen_turned = sem("gen_turned")
        gen_copied = sem("gen_copied")
        gen_multiplied = sem("gen_multiplied")
        gen_summed = sem("gen_summed")
        gen_feat = sem("gen_feat")
        feat_made = sem("feat_made")
        feat_stats = sem("feat_stats")
        last_rstd = sem("last_rstd")
        feat_moments = sem("feat_moments")
        y_stored = sem("y_stored")

        block = ctx.enter_context(nc.Block())

        def chain_on(eng, counter):
            count = [0]

            def step(ins):
                count[0] += 1
                ins.then_inc(counter, 1)
                eng.wait_ge(counter, count[0])
            return step

        def fast(eng):
            eng.wait_ge(flag_made, 1)
            return eng.value_load(flag[0:1, 0:1], min_val=0, max_val=1)

        def over(ap, n):
            return ap.unsqueeze(len(ap.shape)).broadcast_to(list(ap.shape) + [n])

        def combine_rows(v, step, coef):
            hs_b = hsum[:, :].rearrange("p (h c) -> p h c", c=HA).unsqueeze(1).broadcast_to([P, IB, H, HA])
            flat = sums.rearrange("p i h k c -> p (i h k c)")
            rows = sums.rearrange("p i h k c -> p (i h k) c")
            step(v.tensor_tensor(flat, flat, lows.rearrange("p i h k c -> p (i h k c)"), ALU.add))
            step(v.tensor_tensor(rows, rows, over(coef.rearrange("p i h k -> p (i h k)"), HA), ALU.mult))
            step(v.tensor_tensor(uu, sums[:, :, :, 0], sums[:, :, :, 1], ALU.add))
            step(v.tensor_scalar(e0, uu[:, :, :, HD], 0.0, None, ALU.is_equal))
            step(v.tensor_tensor(vv, hs_b, over(e0, HA), ALU.mult))
            step(v.tensor_tensor(uu, uu, vv, ALU.add))
            if v is nc.vector:
                step(nc.vector.reciprocal(e0, uu[:, :, :, HD]))
            else:
                step(v.tensor_tensor(e0, uu[:, :, :, HD], mone.rearrange("p (i h) -> p i h", h=H), ALU.pow))
            return lambda: v.tensor_tensor(feat.rearrange("p i (h c) -> p i h c", c=HD), uu[:, :, :, 0:HD], over(e0, HD), ALU.mult)

        def rstd_rows(step, buf):
            mv, lnst = buf["mv"], buf["lnst"]
            step(nc.gpsimd.tensor_tensor(lnst[:, 0], mv[:, :, 1], epsc[:, 0:IB], ALU.add))
            return lambda: nc.gpsimd.tensor_tensor(lnst[:, 1], lnst[:, 0], mhalf[:, 0:IB], ALU.pow)

        def layernorm_rows(v, step, buf, half, rstd_ready):
            feat, mv, lnst = (buf[k] for k in ("feat", "mv", "lnst"))
            step(v.tensor_tensor(feat, feat, over(mv[:, :, 0], F), ALU.subtract))
            rstd_ready()
            step(v.tensor_tensor(feat, feat, over(lnst[:, 1], F), ALU.mult))
            step(v.tensor_tensor(feat, feat, gam[:, :].unsqueeze(1).broadcast_to([P, IB, F]), ALU.mult))
            step(v.tensor_tensor(feat, feat, bet[:, :].unsqueeze(1).broadcast_to([P, IB, F]), ALU.add))
            return lambda: v.tensor_tensor(buf["yout"], feat, buf["x_res"][:, half], ALU.add)

        @block.sync
        def _(sp):
            x_v = x.rearrange("(t p) f -> p t f", p=P)
            sp.dma_start(Wsb, W).then_inc(w_loaded, 16)
            sp.wait_ge(asd_clear, 1)
            a_v = a.rearrange("(k d) o -> k d o", k=2)
            for h in range(H):
                for k in range(2):
                    sp.dma_start(Asd[h * HD:(h + 1) * HD, k * H + h:k * H + h + 1], a_v[k]).then_inc(a_loaded, 16)
            for g in range(1, SSTEPS):
                sp.dma_start(xin[:, g * SG:(g + 1) * SG], x_v[:, g * SG:(g + 1) * SG, :]).then_inc(x_loaded[g], 16)
            sp.dma_start(gam[:, :], gamma.partition_broadcast(P)).then_inc(consts_loaded, 16)
            sp.dma_start(bet[:, :], beta.partition_broadcast(P)).then_inc(consts_loaded, 16)
            sp.wait_ge(s_copied, 1)
            sp.dma_start(sd_dram.rearrange("(k h) (t p) -> (h t) k p", p=P, k=4), sd_st).then_inc(sd_stored, 16)
            sp.wait_ge(sd_stored, 16)
            adj_v = adj.rearrange("(b i p) j -> b p i j", i=IB, p=P)
            adj_t = adj.rearrange("(t p) j -> t p j", p=P)
            xr_v = x.rearrange("(b i p) f -> b p i f", i=IB, p=P)

            def block_loads(b, half):
                sp.wait_ge(acc_read, b + 1)
                sp.dma_start(s_rows[:, half], sd_dram[0:H, bass.ds(b * BI, BI)].partition_broadcast(P)).then_inc(rows_loaded[half], 16)
                with sp.Fori(0, LOADS // NBUF) as q:
                    for k in range(NBUF):
                        sp.wait_ge(tile_turned, b * CHUNKS + q * (NBUF * CPL) + (k + 1) * CPL)
                        sp.dma_start(adj_in[:, k], adj_v[b][:, :, bass.ds(q * (NBUF * LJ * P) + k * LJ * P, LJ * P)]).then_inc(adj_loaded[k], 16)
                sp.wait_ge(hsum_copied, 1)
                sp.dma_start(x_res[:, half], xr_v[b]).then_inc(x_res_loaded[half], 16)

            def general():
                sp.wait_ge(coefs_made, 1)
                sp.wait_ge(flag_made, 1)
                with sp.Fori(0, BLOCKS) as b:
                    sp.wait_ge(acc_read, b + 2)
                    sp.dma_start(ln_gen["x_res"][:, 0], xr_v[b]).then_inc(x_res_loaded[0], 16)
                    with sp.Fori(0, IB) as i:
                        sp.wait_ge(gen_feat, (b * IB + i) * H + 1)
                        sp.dma_start(cap, adj_t[b * IB + i]).then_inc(gen_adj, 16)
                        with sp.Fori(0, H) as h:
                            for c in range(2):
                                sp.wait_ge(gen_d_used, ((b * IB + i) * H + h) * 2 + (c + 1))
                                sp.dma_start(d_rows, sd_dram[bass.ds(h + H, 1), c * DC:(c + 1) * DC].partition_broadcast(P)).then_inc(gen_d, 16)

            takes = fast(sp)
            with sp.If(takes > 0):
                with sp.Fori(0, BLOCKS // 2) as bp:
                    for half in range(2):
                        block_loads(bp * 2 + half, half)
            with sp.Else():
                general()

        @block.gpsimd
        def _(pool):
            def chain():
                return chain_on(pool, pool_step)

            nc.gpsimd.memset(Asd, 0.0).then_inc(asd_clear, 1)
            nc.gpsimd.memset(mhalf, -0.5)
            nc.gpsimd.memset(epsc, EPS)
            nc.gpsimd.memset(ident[:, :], 0.0).then_inc(pool_step, 1)
            pool.wait_ge(pool_step, 1)
            nc.gpsimd.affine_select(out=ident[:, :], in_=ident[:, :], compare_op=ALU.not_equal, fill=1.0,
                                    base=0, pattern=[[-1, P]], channel_multiplier=1).then_inc(pool_step, 1)
            pool.wait_ge(pool_step, 2)
            pool.sem_clear(pool_step)
            nc.gpsimd.tensor_copy(ident16[:, :], ident[:, :]).then_inc(consts_made, 1)
            nc.gpsimd.memset(mone, -1.0)
            nc.gpsimd.memset(zero16[:, :], 0.0)
            nc.gpsimd.memset(ones[:, :], 1.0)
            nc.gpsimd.memset(haug[:, :, :, HD:HA], 1.0).then_inc(ones_made, 1)
            for g in range(SSTEPS):
                ts = slice(g * SG, (g + 1) * SG)
                pool.wait_ge(moments_made, g + 1)
                step = chain()
                step(nc.gpsimd.tensor_tensor(vpe[:, ts], mv[:, ts, 1], epsc, ALU.add))
                step(nc.gpsimd.tensor_tensor(rstd[:, ts], vpe[:, ts], mhalf, ALU.pow))
                step(nc.gpsimd.tensor_tensor(nmr[:, ts], mv[:, ts, 0], rstd[:, ts], ALU.mult))
                pool.sem_clear(pool_step)
                nc.gpsimd.tensor_scalar(nmr[:, ts], nmr[:, ts], -1.0, None, ALU.mult).then_inc(norm_made, 1)
            pool.wait_ge(col_max, 3)
            nc.gpsimd.partition_all_reduce(small[:, 16:16 + 2 * H + 1], small[:, 0:2 * H + 1], P, RMAX).then_inc(all_max, 1)

            pool.wait_ge(consts_loaded, 32)
            pool.sem_inc(acc_read, 2)
            out_v = out.rearrange("(b i p) f -> b p i f", i=IB, p=P)

            def finish(b, half, buf):
                pool.wait_ge(feat_moments, b + 2)
                step = chain()
                last = layernorm_rows(nc.gpsimd, step, buf, half, lambda: step(rstd_rows(step, buf)()))
                pool.sem_clear(pool_step)
                last().then_inc(acc_read, 1)
                pool.wait_ge(acc_read, b + 3)
                pool.dma_start(out_v[b], buf["yout"]).then_inc(y_stored, 16)
                pool.wait_ge(y_stored, b * 16 + 16)

            def combine(b):
                pool.wait_ge(acc_copied, b * 2 + 4)
                last = combine_rows(nc.gpsimd, chain(), coefs[:, bass.ds(b * IB, IB)])
                pool.sem_clear(pool_step)
                last().then_inc(feat_made, 1)

            takes = fast(pool)
            with pool.If(takes > 0):
                pool.wait_ge(hsum_copied, 1)
                pool.wait_ge(coefs_made, 1)
                nc.gpsimd.memset(feat, 0.0).then_inc(feat_made, 1)
                with pool.Fori(0, BLOCKS // 2 - 1) as bp:
                    for half in range(2):
                        pool.wait_ge(x_res_loaded[half], bp * 16 + 16)
                        combine(bp * 2 + half)
                        finish(bp * 2 + half, half, ln_fast)
                pool.wait_ge(x_res_loaded[0], 8 * BLOCKS)
                combine(BLOCKS - 2)
                finish(BLOCKS - 2, 0, ln_fast)
                pool.wait_ge(feat_moments, BLOCKS + 1)
                last = rstd_rows(chain(), ln_fast)
                pool.sem_clear(pool_step)
                last().then_inc(last_rstd, 1)
                pool.wait_ge(acc_read, BLOCKS + 2)
                pool.dma_start(out_v[BLOCKS - 1], ln_fast["yout"]).then_inc(y_stored, 16)
                pool.wait_ge(y_stored, 16 * BLOCKS)
            with pool.Else():
                with pool.Fori(0, BLOCKS) as b:
                    pool.wait_ge(x_res_loaded[0], b * 16 + 16)
                    finish(b, 0, ln_gen)

        @block.vector
        def _(dve):
            dve.sem_inc(masks_made, DEEP)
            dve.sem_inc(maskA_made, 1)

            dve.wait_ge(wt_turned, 1)
            nc.vector.tensor_copy(WT, pmisc[:, 0:F]).then_inc(wt_copied, 1)
            dve.wait_ge(wa_made, 1)
            nc.vector.tensor_copy(WA, pmisc[:, F:F + 2 * H]).then_inc(wa_copied, 1)

            def stats_of(g):
                dve.wait_ge(x_loaded[g], 16)
                for t in range(g * SG, (g + 1) * SG):
                    last = nc.vector.bn_stats(stats[:, t], xin[:, t])
                last.then_inc(stats_made, 1)
                dve.wait_ge(stats_made, g + 1)
                for t in range(g * SG, (g + 1) * SG):
                    last = nc.vector.bn_aggr(mv[:, t], stats[:, t])
                last.then_inc(moments_made, 1)

            for g in range(AHEAD):
                stats_of(g)

            def max_h(st):
                dve.wait_ge(h_copied, st + 1)
                nc.vector.tensor_reduce(hmax[:, st:st + 1], haug[:, st * PG:(st + 1) * PG, :, 0:HD], axis=AX.XYZ, op=ALU.max,
                                        apply_absolute_value=True).then_inc(hmax_made, 1)

            LAG = 2
            for st in range(PSTEPS + LAG):
                if st < PSTEPS:
                    dve.wait_ge(hn_turned, st + 1)
                    if st >= 2:
                        dve.wait_ge(h_made, st - 1)
                    for i in range(2):
                        last = nc.vector.tensor_copy(hnT[:, st % 2, 4 * i:4 * i + 4],
                                                     ptr[st % 2][i][:, :].rearrange("p (t n) -> p t n", n=P))
                    last.then_inc(hnT_copied, 1)
                if st + AHEAD < SSTEPS:
                    stats_of(st + AHEAD)
                if st >= LAG:
                    max_h(st - LAG)

            dve.wait_ge(h_copied, PSTEPS)
            dve.wait_ge(hmax_made, PSTEPS)
            nc.vector.tensor_reduce(small[:, 0:H], sd[:, H:2 * H, :], axis=AX.X, op=ALU.max).then_inc(col_max, 1)
            nc.vector.tensor_reduce(small[:, H:2 * H], sd[:, H:2 * H, :], axis=AX.X, op=ALU.min, negate=True).then_inc(col_max, 1)
            nc.vector.tensor_reduce(small[:, 2 * H:2 * H + 1], hmax, axis=AX.X, op=ALU.max).then_inc(col_max, 1)
            dve.wait_ge(s_turned, 1)
            nc.vector.tensor_copy(sd_st, pmisc[:, 0:4 * P].rearrange("p (k n) -> p k n", n=P)).then_inc(s_copied, 1)
            nc.vector.tensor_scalar(negd[:, :, :].rearrange("p t h -> p h t"), sd[:, H:2 * H, :], -1.0, None, ALU.mult)
            dve.wait_ge(all_max, 1)
            nc.vector.tensor_scalar(small[:, 56:60], small[:, 16:16 + H], -1.0, SCALE, ALU.mult, ALU.add)
            nc.vector.tensor_scalar(small[:, 60:64], small[:, 16:16 + H], -SLOPE, SCALE, ALU.mult, ALU.add).then_inc(bias_made, 1)
            for h in range(H):
                nc.vector.tensor_scalar(yv[:, 0, h], sd[:, h, :], small[:, 16 + h:17 + h], 0.0, ALU.add, ALU.min)
                last = nc.vector.tensor_scalar(yv[:, 1, h], sd[:, h, :], small[:, 16 + h:17 + h], 0.0, ALU.add, ALU.max)
            last.then_inc(y_made, 1)
            step = chain_on(dve, dve_step)
            nc.vector.tensor_scalar(small[:, 36:37], small[:, 24:25], H_HIGH, None, ALU.is_le)
            nc.vector.tensor_scalar(small[:, 37:38], small[:, 24:25], H_LOW, None, ALU.is_ge)
            step(nc.vector.tensor_tensor(small[:, 32:36], small[:, 16:16 + H], small[:, 16 + H:16 + 2 * H], ALU.add))
            step(nc.vector.tensor_scalar(small[:, 32:36], small[:, 32:36], RANGE, None, ALU.is_le))
            step(nc.vector.tensor_reduce(small[:, 41:42], small[:, 32:38], axis=AX.X, op=ALU.min))
            nc.vector.tensor_copy(flag[:, :], small[:, 41:42]).then_inc(flag_made, 1)
            dve.sem_clear(dve_step)

            def row_stats(buf):
                for i in range(IB):
                    last = nc.vector.bn_stats(buf["stats"][:, i], buf["feat"][:, i])
                last.then_inc(feat_stats, 1)

            def row_moments(buf):
                dve.wait_ge(feat_stats, 1)
                dve.sem_clear(feat_stats)
                for i in range(IB):
                    last = nc.vector.bn_aggr(buf["mv"][:, i], buf["stats"][:, i])
                last.then_inc(feat_moments, 1)

            def general():
                dve.wait_ge(coefs_made, 1)
                dve.wait_ge(sd_stored, 16)
                dve.sem_inc(gen_d_used, 1)
                dve.sem_inc(gen_feat, 1)
                dve.sem_inc(feat_moments, 1)
                BIG = 9e15
                with dve.Fori(0, BLOCKS) as b:
                    with dve.Fori(0, IB) as i:
                        t = b * IB + i
                        dve.wait_ge(acc_read, b + 2)
                        dve.wait_ge(gen_adj, t * 16 + 16)
                        step = chain_on(dve, dve_step)
                        step(nc.vector.tensor_scalar(cap, cap, 0.0, 2 * BIG, ALU.is_gt, ALU.mult))
                        step(nc.vector.tensor_scalar(cap, cap, -BIG, None, ALU.add))
                        dve.sem_clear(dve_step)
                        with dve.Fori(0, H) as h:
                            m = t * H + h
                            step = chain_on(dve, dve_step)
                            for c in range(2):
                                part = logits[:, c * DC:(c + 1) * DC]
                                dve.wait_ge(gen_d, m * 32 + (c + 1) * 16)
                                nc.vector.tensor_scalar(part, d_rows, sd[:, bass.ds(h, 1), bass.ds(t, 1)].squeeze(2), None,
                                                        ALU.add).then_inc(gen_d_used, 1)
                                dve.wait_ge(gen_d_used, m * 2 + (c + 2))
                                step(nc.vector.scalar_tensor_tensor(part, part, SLOPE, part, ALU.mult, ALU.max))
                                step(nc.vector.tensor_tensor(part, part, cap[:, c * DC:(c + 1) * DC], ALU.min))
                            nc.vector.tensor_reduce(neg_max, logits, axis=AX.X, op=ALU.max, negate=True).then_inc(gen_logits, 1)
                            dve.sem_clear(dve_step)
                            for g in range(GROUPS):
                                dve.wait_ge(gen_turned, m * GROUPS + (g + 1))
                                if g >= 2:
                                    dve.wait_ge(gen_multiplied, m * GROUPS + (g - 1))
                                nc.vector.tensor_copy(probsT[:, g % 2], bank[6 + g % 2][:, :]).then_inc(gen_copied, 1)
                            dve.wait_ge(gen_summed, m + 1)
                            step = chain_on(dve, dve_step)
                            step(nc.vector.reciprocal(inv_denom, denom))
                            dve.sem_clear(dve_step)
                            nc.vector.tensor_scalar(ln_gen["feat"][:, bass.ds(i, 1), bass.ds(h * HD, HD)].squeeze(1), bank[0][:, 0:HD],
                                                    inv_denom, None, ALU.mult).then_inc(gen_feat, 1)
                    dve.wait_ge(gen_feat, b * (IB * H) + (IB * H + 1))
                    row_stats(ln_gen)
                    row_moments(ln_gen)

            takes = fast(dve)
            with dve.If(takes > 0):
                dve.wait_ge(exps_made, 1)
                nc.vector.tensor_scalar(expU[:, :, :], expU[:, :, :], -1.0, None, ALU.mult).then_inc(expU_negated, 1)
                dve.wait_ge(expU_negated, 1)

                with dve.Fori(0, WSTEPS // 2) as g2:
                    for q in range(2):
                        g = g2 * 2 + q
                        for k, ex in enumerate((expU, expV)):
                            nc.vector.tensor_tensor(xw[2 * q + k], haug[:, bass.ds(g * WG, WG)],
                                                    ex[:, bass.ds(g * WG, WG), :].unsqueeze(3).broadcast_to([P, WG, H, HA]),
                                                    ALU.mult).then_inc(scaled, 1)
                    for q in range(2):
                        g = g2 * 2 + q
                        for k in range(2):
                            dve.wait_ge(hi_made, g * 2 + (k + 1))
                            nc.vector.scalar_tensor_tensor(weights[:, bass.ds(g * WG, WG), :, (2 * k + 1) * HA:(2 * k + 2) * HA],
                                                           weights[:, bass.ds(g * WG, WG), :, 2 * k * HA:(2 * k + 1) * HA], -LO,
                                                           xw[2 * q + k], ALU.mult, ALU.add).then_inc(lo_made, 1)
                    dve.wait_ge(lo_made, g2 * 4 + 4)
                dve.wait_ge(hsum_made, 1)
                nc.vector.tensor_copy(hsum[:, :], pmisc[:, 0:H * HA]).then_inc(hsum_copied, 1)

                dve.wait_ge(coefs_made, 1)
                dve.wait_ge(sd_stored, 16)

                def edges(c, k):
                    dve.wait_ge(tile_turned, c + (2 * NBUF + 1))
                    dve.wait_ge(masks_used, c + 1)
                    nc.vector.tensor_scalar(maskA[:, k % DEEP], turned[k % 2], 0.0, 1.0, ALU.is_le, ALU.subtract).then_inc(maskA_made, 1)

                def masks(c, k, half, next_edges=True):
                    dve.wait_ge(masks_used, c + (DEEP - 1))
                    dve.wait_ge(maskA_made, c + 2)
                    for u in range(CJ):
                        jt = k * CJ + u
                        nc.vector.scalar_tensor_tensor(maskB[:, k % 2, 0, u], s_rows[:, half, 0], negd[:, jt:jt + 1, 0],
                                                       maskA[:, k % DEEP, u], ALU.is_lt, ALU.logical_and)
                    if next_edges:
                        edges(c + 1, k + 1)
                    dve.wait_ge(below_made, c + 1)
                    nc.vector.tensor_tensor(maskB[:, k % 2, H - ZH:H].rearrange("p h u i -> p h (u i)"),
                                            below[:, k % DEEP].rearrange("p h u i -> p h (u i)"),
                                            maskA[:, k % DEEP].rearrange("p u i -> p (u i)").unsqueeze(1).broadcast_to([P, ZH, CJ * BI]),
                                            ALU.logical_and).then_inc(masks_made, 1)

                def flush(b):
                    dve.wait_ge(masks_used, b * CHUNKS + DEEP)
                    dve.wait_ge(acc_read, b + 1)
                    for dst, src in copies(sums, 0, 1):
                        nc.vector.tensor_copy(dst, src)
                    for dst, src in copies(lows, 1, 1):
                        last = nc.vector.tensor_scalar(dst, src, 1.0 / LO, None, ALU.mult)
                    last.then_inc(acc_copied, 1)

                def attend(b, half, loads, last=False):
                    dve.wait_ge(rows_loaded[half], loads)
                    for k in range(CHUNKS):
                        masks(b * CHUNKS + k, k, half, next_edges=not (last and k == CHUNKS - 1))
                        if k == 0:
                            flush(b)
                        if k == STATS_AT:
                            dve.wait_ge(feat_made, b + 1)
                            row_stats(ln_fast)
                        if k == STATS_AT + 1:
                            row_moments(ln_fast)

                edges(0, 0)
                with dve.Fori(0, BLOCKS // 2 - 1) as bp:
                    for half in range(2):
                        attend(bp * 2 + half, half, bp * 16 + 16)
                for half in range(2):
                    attend(BLOCKS - 2 + half, half, 8 * BLOCKS, last=half == 1)
                flush(BLOCKS)
                dve.wait_ge(acc_copied, 2 * BLOCKS + 2)
                dve.wait_ge(x_res_loaded[1], 8 * BLOCKS)
                dve.wait_ge(y_stored, 16 * (BLOCKS - 1))
                last = combine_rows(nc.vector, chain_on(dve, dve_step), coefs[:, (BLOCKS - 1) * IB:BLOCKS * IB])
                dve.sem_clear(dve_step)
                last().then_inc(feat_made, 1)
                dve.wait_ge(feat_made, BLOCKS + 1)
                row_stats(ln_fast)
                row_moments(ln_fast)
                dve.wait_ge(feat_moments, BLOCKS + 1)
                last = layernorm_rows(nc.vector, chain_on(dve, dve_step), ln_fast, 1, lambda: dve.wait_ge(last_rstd, 1))
                dve.sem_clear(dve_step)
                last().then_inc(acc_read, 1)
            with dve.Else():
                general()

        @block.scalar
        def _(act):
            act.dma_start(xin[:, 0:SG], x.rearrange("(t p) f -> p t f", p=P)[:, 0:SG, :]).then_inc(x_loaded[0], 16)
            LAG = 2
            for st in range(PSTEPS + LAG):
                if st < PSTEPS:
                    act.wait_ge(norm_made, st * PG // SG + 1)
                    for t in range(st * PG, (st + 1) * PG):
                        last = nc.scalar.activation(hn[:, t], xin[:, t], ACT.Relu, bias=nmr[:, t:t + 1], scale=rstd[:, t:t + 1])
                    last.then_inc(hn_made, 1)
                if st >= LAG:
                    t0 = (st - LAG) * PG
                    act.wait_ge(h_made, st - LAG + 1)
                    for i in range(2):
                        nc.scalar.activation(haug[:, t0 + 4 * i:t0 + 4 * i + 4, :, 0:HD],
                                             ph[i][:, :].rearrange("p (t h c) -> p t h c", h=H, c=HD), ACT.Copy)
                    nc.scalar.activation(sd[:, :, t0:t0 + PG], psd[:, 0:PG * 2 * H].rearrange("p (t c) -> p c t", c=2 * H),
                                         ACT.Copy).then_inc(h_copied, 1)

            act.wait_ge(bias_made, 1)
            for h in range(H):
                nc.scalar.activation(expU[:, :, h], sd[:, H + h, :], ACT.Exp, bias=small[:, 56 + h:57 + h])
                last = nc.scalar.activation(expV[:, :, h], sd[:, H + h, :], ACT.Exp, bias=small[:, 60 + h:61 + h], scale=SLOPE)
            last.then_inc(exps_made, 1)
            act.wait_ge(y_made, 1)
            nc.scalar.activation(coefs[:, :, :, 0].rearrange("p t h -> p h t"), yv[:, 0], ACT.Exp, scale=1.0 - SLOPE)
            nc.scalar.activation(coefs[:, :, :, 1].rearrange("p t h -> p h t"), yv[:, 1], ACT.Exp, scale=SLOPE - 1.0).then_inc(coefs_made, 1)
            def general():
                with act.Fori(0, NT * H) as m:
                    act.wait_ge(gen_logits, m + 1)
                    nc.scalar.activation(probs, logits, ACT.Exp, bias=neg_max, accum_out=denom).then_inc(gen_probs, 1)

            takes = fast(act)
            with act.If(takes > 0):
                with act.Fori(0, WSTEPS // 2) as g2:
                    for q in range(2):
                        for k in range(2):
                            act.wait_ge(scaled, g2 * 4 + (2 * q + k + 1))
                            nc.scalar.activation(weights[:, bass.ds((g2 * 2 + q) * WG, WG), :, 2 * k * HA:(2 * k + 1) * HA],
                                                 xw[2 * q + k], ACT.Copy, scale=1.0 / LO).then_inc(hi_made, 1)

                def flush(b):
                    act.wait_ge(masks_used, b * CHUNKS + DEEP)
                    act.wait_ge(acc_read, b + 1)
                    for dst, src in copies(sums, 0, 0):
                        nc.scalar.activation(dst, src, ACT.Copy)
                    for dst, src in copies(lows, 1, 0):
                        last = nc.scalar.activation(dst, src, ACT.Copy, scale=1.0 / LO)
                    last.then_inc(acc_copied, 1)

                def compare(c, k, half):
                    act.wait_ge(masks_made, c + 1)
                    for u in range(CJ):
                        for z in range(ZH):
                            h = H - ZH + z
                            last = nc.scalar.activation(below[:, k % DEEP, z, u], s_rows[:, half, h], ACT.Relu,
                                                        bias=negd[:, k * CJ + u:k * CJ + u + 1, h], scale=-1.0)
                    last.then_inc(below_made, 1)

                with act.Fori(0, BLOCKS // 2) as bp:
                    for half in range(2):
                        b = bp * 2 + half
                        act.wait_ge(rows_loaded[half], bp * 16 + 16)
                        for k in range(CHUNKS):
                            compare(b * CHUNKS + k, k, half)
                            if k == FLUSH_AT:
                                if half == 0:
                                    act.wait_ge(hsum_copied, 1)
                                flush(b)
                flush(BLOCKS)
            with act.Else():
                general()

        @block.tensor
        def _(pe):
            pe.sem_inc(tile_turned, 2 * NBUF)
            pe.wait_ge(consts_made, 1)
            pe.wait_ge(w_loaded, 16)
            nc.tensor.transpose(pmisc[:, 0:F], Wsb, ident[:, :]).then_inc(wt_turned, 1)
            pe.wait_ge(wt_copied, 1)
            pe.wait_ge(a_loaded, 16 * 2 * H)
            nc.tensor.matmul(pmisc[:, F:F + 2 * H], WT, Asd, start=True, stop=True).then_inc(wa_made, 1)
            pe.wait_ge(wa_copied, 1)

            def turn_rows(st):
                pe.wait_ge(hn_made, st + 1)
                if st >= 2:
                    pe.wait_ge(hnT_copied, st - 1)
                for t in range(PG):
                    last = nc.tensor.transpose(ptr[st % 2][t // 4][:, (t % 4) * P:(t % 4 + 1) * P], hn[:, st * PG + t], ident[:, :])
                last.then_inc(hn_turned, 1)

            turn_rows(0)
            for st in range(PSTEPS):
                if st + 1 < PSTEPS:
                    turn_rows(st + 1)
                pe.wait_ge(hnT_copied, st + 1)
                if st >= 1:
                    pe.wait_ge(h_copied, st)
                for t in range(PG):
                    nc.tensor.matmul(ph[t // 4][:, (t % 4) * F:(t % 4 + 1) * F], hnT[:, st % 2, t], Wsb, start=True, stop=True)
                    last = nc.tensor.matmul(psd[:, t * 2 * H:(t + 1) * 2 * H], hnT[:, st % 2, t], WA, start=True, stop=True)
                last.then_inc(h_made, 1)
            pe.wait_ge(h_copied, PSTEPS)
            for k in range(4):
                last = nc.tensor.transpose(pmisc[:, k * P:(k + 1) * P], sd[:, 2 * k:2 * k + 2, :].rearrange("p h t -> p (h t)"), ident[:, :])
            last.then_inc(s_turned, 1)
            def general():
                with pe.Fori(0, BLOCKS * IB) as t:
                    with pe.Fori(0, H) as h:
                        m = t * H + h
                        pe.wait_ge(gen_probs, m + 1)

                        def turn_probs(g):
                            if g >= 2:
                                pe.wait_ge(gen_copied, m * GROUPS + (g - 1))
                            for u in range(TG):
                                j = (g * TG + u) * P
                                last = nc.tensor.transpose(bank[6 + g % 2][:, u * P:(u + 1) * P], probs[:, j:j + P], ident[:, :])
                            last.then_inc(gen_turned, 1)

                        turn_probs(0)
                        for g in range(GROUPS):
                            if g + 1 < GROUPS:
                                turn_probs(g + 1)
                            pe.wait_ge(gen_copied, m * GROUPS + (g + 1))
                            for u in range(TG):
                                last = nc.tensor.matmul(bank[0][:, 0:HD], probsT[:, g % 2, u * P:(u + 1) * P],
                                                        haug[:, g * TG + u, bass.ds(h, 1), 0:HD].squeeze(1),
                                                        start=g + u == 0, stop=g * TG + u == NT - 1)
                            last.then_inc(gen_multiplied, 1)
                        pe.drain().then_inc(gen_summed, 1)

            takes = fast(pe)
            with pe.If(takes > 0):
                pe.wait_ge(s_copied, 1)
                pe.wait_ge(ones_made, 1)
                for t in range(NT):
                    last = nc.tensor.matmul(pmisc[:, 0:H * HA], ones[:, :], hbig[:, t * H * HA:(t + 1) * H * HA],
                                            start=t == 0, stop=t == NT - 1)
                last.then_inc(hsum_made, 1)
                pe.wait_ge(hsum_copied, 1)

                def turn(slot, k, cc):
                    a16 = adj_in[:, k].bitcast(bf16)
                    for u in range(CJ):
                        for it in range(IB):
                            j0 = 2 * (cc * CJ + u) * P
                            last = nc.tensor.transpose(turned[slot][:, u, it * P:(it + 1) * P],
                                                       a16[:, it, j0 + 1:j0 + 2 * P:2], ident16[:, :])
                    last.then_inc(tile_turned, 1)

                def clear():
                    for i in range(IB + IB // 2):
                        used = (3 if i < IB else 2) * WC
                        last = nc.tensor.matmul(bank[i][:, 0:used], zero16[0:1, 0:P], zero16[0:1, 0:used], start=True, stop=False,
                                                skip_group_check=True)
                    return last

                def products(c, k):
                    pe.wait_ge(masks_made, c + (DEEP + 1))
                    for u in range(CJ):
                        w = weights[:, k * CJ + u]
                        for it in range(IB):
                            cols = slice(it * P, (it + 1) * P)
                            mA = maskA[:, k % DEEP, u, cols]
                            nc.tensor.matmul(accA[it][:, :, 0:2 * HA], mA, w[:, 0:3, 0:2 * HA], start=False, stop=False,
                                             skip_group_check=True)
                            nc.tensor.matmul(accB[it // 2][:, it % 2, 0:2 * HA], mA, w[:, 3, 0:2 * HA], start=False, stop=False,
                                             skip_group_check=True)
                            for h in range(H):
                                last = nc.tensor.matmul(acc(it, h), maskB[:, k % 2, h, u, cols], w[:, h], start=False, stop=False,
                                                        skip_group_check=True)
                    last.then_inc(masks_used, 1)

                def attend(b, last=False):
                    for k in range(CHUNKS):
                        ahead = k + 2
                        load, part = divmod(ahead, CPL)
                        if not (last and ahead >= CHUNKS):
                            if part == 0:
                                pe.wait_ge(adj_loaded[load % NBUF], b * (16 * LOADS // NBUF) + 16 * (load // NBUF + 1))
                            pe.wait_ge(maskA_made, b * CHUNKS + (k + 2))
                            turn(ahead % 2, load % NBUF, part)
                        if k == 0:
                            pe.wait_ge(acc_copied, b * 2 + 2)
                            clear()
                        products(b * CHUNKS + k, k)

                clear().then_inc(masks_used, DEEP)
                pe.wait_ge(adj_loaded[0], 16)
                turn(0, 0, 0)
                turn(1, 0, 1)
                with pe.Fori(0, BLOCKS - 1) as b:
                    attend(b)
                attend(BLOCKS - 1, last=True)
            with pe.Else():
                general()


_INS = ["x", "adj", "L0_gnn_W", "L0_gnn_a", "L0_gnn_gamma", "L0_gnn_beta"]


def kernel(**inputs):
    import numpy as _np
    import concourse.bacc as _bacc
    from concourse import mybir as _mybir
    from concourse.bass_utils import run_bass_kernel_spmd as _run

    nc = _bacc.Bacc("TRN2", target_bir_lowering=False, num_devices=1)
    arrays, args = {}, []
    for name in _INS:
        arr = _np.ascontiguousarray(inputs[name])
        arrays[f"in_{name}_dram"] = arr
        args.append(nc.dram_tensor(f"in_{name}_dram", arr.shape, _mybir.dt.from_np(arr.dtype), kind="ExternalInput").ap())
    o = nc.dram_tensor("out_0_dram", arrays["in_x_dram"].shape, _mybir.dt.float32, kind="ExternalOutput").ap()
    bass_gat_preln_kernel(nc, *args, o)
    r = _run(nc, [arrays], core_ids=[0])
    return r.results[0]["out_0_dram"]
```
